# Optimizing a Trainium2 kernel written in Bass

```python
import numpy as np
import jax
import jax.numpy as jnp

def _softmax(x, axis=-1):
    return jax.nn.softmax(x, axis=axis)

def _gelu(x):
    return jax.nn.gelu(x, approximate=True)

def _silu(x):
    return jax.nn.silu(x)

def _sigmoid(x):
    return jax.nn.sigmoid(x)

def _layernorm(x, axis=-1, eps=1e-05):
    m = jnp.mean(x, axis=axis, keepdims=True)
    v = jnp.var(x, axis=axis, keepdims=True)
    return (x - m) / jnp.sqrt(v + eps)

def _scatter_add(tgt, idx, src, axis=0):
    return tgt.at[idx].add(src)

def _segment_sum(src, seg, n):
    return jax.ops.segment_sum(src, seg, n)
kernel_name = 'mk_conv_seq_d1_conv_nhwc768_r4_406329'

def setup_inputs(seed: int=0):
    np.random.seed(seed)
    _w = jnp.asarray

    def _rec_inputs():
        import jax
        import jax.numpy as jnp
        _gk = jax.random.key(seed)
        x = -0.0002221 + 1 * jax.random.normal(jax.random.fold_in(_gk, 1), (8, 16, 16, 192), jnp.float32)
        return x
    x = _rec_inputs()

    def _L0_conv_setup():
        import jax, jax.numpy as jnp
        import numpy as np
        B, H, W, C = (8, 16, 16, 192)
        HEADS = 12
        KD = C // HEADS
        WS = 14
        MLP_DIM = 768
        EPS = 1e-06

        def layer_norm(x, g, b):
            mu = jnp.mean(x, axis=-1, keepdims=True)
            var = jnp.var(x, axis=-1, keepdims=True)
            return (x - mu) * jax.lax.rsqrt(var + EPS) * g + b
        key = jax.random.key(seed)
        ks = jax.random.split(key, 10)
        s = 0.02
        return {'x': jax.random.normal(ks[0], (B, H, W, C), jnp.float32), 'ln1_g': jnp.ones((C,), jnp.float32), 'ln1_b': jnp.zeros((C,), jnp.float32), 'qkv_w': jax.random.normal(ks[1], (C, 3 * C), jnp.float32) * s, 'qkv_b': jnp.zeros((3 * C,), jnp.float32), 'proj_w': jax.random.normal(ks[2], (C, C), jnp.float32) * s, 'proj_b': jnp.zeros((C,), jnp.float32), 'rel_h': jax.random.normal(ks[3], (2 * WS - 1, KD), jnp.float32) * s, 'rel_w': jax.random.normal(ks[4], (2 * WS - 1, KD), jnp.float32) * s, 'ln2_g': jnp.ones((C,), jnp.float32), 'ln2_b': jnp.zeros((C,), jnp.float32), 'mlp_w1': jax.random.normal(ks[5], (C, MLP_DIM), jnp.float32) * s, 'mlp_b1': jnp.zeros((MLP_DIM,), jnp.float32), 'mlp_w2': jax.random.normal(ks[6], (MLP_DIM, C), jnp.float32) * s, 'mlp_b2': jnp.zeros((C,), jnp.float32)}
    _L0_conv_all = _L0_conv_setup()
    _L0_conv_in = {k: v for k, v in _L0_conv_all.items() if k in ('ln1_g', 'ln1_b', 'qkv_w', 'qkv_b', 'proj_w', 'proj_b', 'rel_h', 'rel_w', 'ln2_g', 'ln2_b', 'mlp_w1', 'mlp_b1', 'mlp_w2', 'mlp_b2')}
    del _L0_conv_all
    return {'x': x, 'L0_conv_ln1_g': _L0_conv_in['ln1_g'], 'L0_conv_ln1_b': _L0_conv_in['ln1_b'], 'L0_conv_qkv_w': _L0_conv_in['qkv_w'], 'L0_conv_qkv_b': _L0_conv_in['qkv_b'], 'L0_conv_proj_w': _L0_conv_in['proj_w'], 'L0_conv_proj_b': _L0_conv_in['proj_b'], 'L0_conv_rel_h': _L0_conv_in['rel_h'], 'L0_conv_rel_w': _L0_conv_in['rel_w'], 'L0_conv_ln2_g': _L0_conv_in['ln2_g'], 'L0_conv_ln2_b': _L0_conv_in['ln2_b'], 'L0_conv_mlp_w1': _L0_conv_in['mlp_w1'], 'L0_conv_mlp_b1': _L0_conv_in['mlp_b1'], 'L0_conv_mlp_w2': _L0_conv_in['mlp_w2'], 'L0_conv_mlp_b2': _L0_conv_in['mlp_b2']}

def reference(x, L0_conv_ln1_g, L0_conv_ln1_b, L0_conv_qkv_w, L0_conv_qkv_b, L0_conv_proj_w, L0_conv_proj_b, L0_conv_rel_h, L0_conv_rel_w, L0_conv_ln2_g, L0_conv_ln2_b, L0_conv_mlp_w1, L0_conv_mlp_b1, L0_conv_mlp_w2, L0_conv_mlp_b2):
    import jax
    import jax.numpy as jnp

    def _L0_conv_ref(x, ln1_g, ln1_b, qkv_w, qkv_b, proj_w, proj_b, rel_h, rel_w, ln2_g, ln2_b, mlp_w1, mlp_b1, mlp_w2, mlp_b2):
        import jax, jax.numpy as jnp
        import numpy as np
        B, H, W, C = (8, 16, 16, 192)
        HEADS = 12
        KD = C // HEADS
        WS = 14
        MLP_DIM = 768
        EPS = 1e-06

        def layer_norm(x, g, b):
            mu = jnp.mean(x, axis=-1, keepdims=True)
            var = jnp.var(x, axis=-1, keepdims=True)
            return (x - mu) * jax.lax.rsqrt(var + EPS) * g + b
        shortcut = x
        h = layer_norm(x, ln1_g, ln1_b)
        pad_h = -H % WS
        pad_w = -W % WS
        hp = jnp.pad(h, ((0, 0), (0, pad_h), (0, pad_w), (0, 0)))
        Hp, Wp = (H + pad_h, W + pad_w)
        nh, nw = (Hp // WS, Wp // WS)
        win = hp.reshape(B, nh, WS, nw, WS, C).transpose(0, 1, 3, 2, 4, 5)
        win = win.reshape(B * nh * nw, WS, WS, C)
        Bw = B * nh * nw
        N = WS * WS
        qkv = win.reshape(Bw, N, C) @ qkv_w + qkv_b
        qkv = qkv.reshape(Bw, N, 3, HEADS, KD).transpose(2, 0, 3, 1, 4)
        qkv = qkv.reshape(3, Bw * HEADS, N, KD)
        q, k, v = (qkv[0], qkv[1], qkv[2])
        scale = KD ** (-0.5)
        attn = jnp.einsum('bnd,bmd->bnm', q * scale, k)
        coords = jnp.arange(WS)[:, None] - jnp.arange(WS)[None, :] + (WS - 1)
        Rh = rel_h[coords]
        Rw = rel_w[coords]
        rq = q.reshape(Bw * HEADS, WS, WS, KD)
        bias_h = jnp.einsum('bhwc,hkc->bhwk', rq, Rh)
        bias_w = jnp.einsum('bhwc,wkc->bhwk', rq, Rw)
        attn = attn.reshape(Bw * HEADS, WS, WS, WS, WS)
        attn = attn + bias_h[..., :, None] + bias_w[..., None, :]
        attn = jax.nn.softmax(attn.reshape(Bw * HEADS, N, N), axis=-1)
        o = attn @ v
        o = o.reshape(Bw, HEADS, WS, WS, KD).transpose(0, 2, 3, 1, 4)
        o = o.reshape(Bw, WS, WS, C) @ proj_w + proj_b
        o = o.reshape(B, nh, nw, WS, WS, C).transpose(0, 1, 3, 2, 4, 5)
        o = o.reshape(B, Hp, Wp, C)[:, :H, :W, :]
        x2 = shortcut + o
        h2 = layer_norm(x2, ln2_g, ln2_b)
        m = jax.nn.gelu(h2 @ mlp_w1 + mlp_b1, approximate=False) @ mlp_w2 + mlp_b2
        return x2 + m

    def _gn(v, G=32, eps=1e-05):
        B_, H_, W_, C_ = v.shape
        g = v.reshape(B_, H_, W_, G, C_ // G)
        m = jnp.mean(g, axis=(1, 2, 4), keepdims=True)
        s = jnp.var(g, axis=(1, 2, 4), keepdims=True)
        return ((g - m) / jnp.sqrt(s + eps)).reshape(v.shape)

    def _ln_c(v, eps=1e-06):
        m = jnp.mean(v, axis=-1, keepdims=True)
        s = jnp.var(v, axis=-1, keepdims=True)
        return (v - m) / jnp.sqrt(s + eps)

    def _ln_t(v, eps=1e-05):
        m = jnp.mean(v, axis=-1, keepdims=True)
        s = jnp.var(v, axis=-1, keepdims=True)
        return (v - m) / jnp.sqrt(s + eps)

    def _to_tokens(v):
        B_, H_, W_, C_ = v.shape
        return v.reshape(B_, H_ * W_, C_)

    def _from_tokens(t, like):
        return t.reshape(like.shape)
    x = _L0_conv_ref(x, L0_conv_ln1_g, L0_conv_ln1_b, L0_conv_qkv_w, L0_conv_qkv_b, L0_conv_proj_w, L0_conv_proj_b, L0_conv_rel_h, L0_conv_rel_w, L0_conv_ln2_g, L0_conv_ln2_b, L0_conv_mlp_w1, L0_conv_mlp_b1, L0_conv_mlp_w2, L0_conv_mlp_b2)
    return x

_drawn_inputs = setup_inputs


def setup_inputs(seed=0):
    import zlib

    import numpy as np

    out = dict(_drawn_inputs(seed))
    spreads = {'L0_conv_ln1_g': (1.0, 0.6),
     'L0_conv_ln1_b': (0.0, 0.8),
     'L0_conv_qkv_b': (0.0, 0.283),
     'L0_conv_proj_b': (0.0, 0.1),
     'L0_conv_ln2_g': (1.0, 0.6),
     'L0_conv_ln2_b': (0.0, 0.8),
     'L0_conv_mlp_b1': (0.0, 0.279),
     'L0_conv_mlp_b2': (0.0, 0.1)}
    factors = {'L0_conv_qkv_w': 6.735, 'L0_conv_rel_h': 8.0, 'L0_conv_rel_w': 8.0}
    for name, (base, spread) in spreads.items():
        noise = np.random.default_rng([zlib.crc32(name.encode()), seed]).standard_normal(out[name].shape)
        drawn = base * np.exp(spread * noise) if base else spread * noise
        out[name] = jnp.asarray(drawn.astype(out[name].dtype))
    for name, factor in factors.items():
        out[name] = (out[name] * factor).astype(out[name].dtype)
    return out
```

```python
from contextlib import ExitStack

import concourse.bass as bass
from concourse import mybir

F32 = mybir.dt.float32
F32R = mybir.dt.float32r
ACT = mybir.ActivationFunctionType
ALU = mybir.AluOpType
AX = mybir.AxisListType

B, H, W, C = 8, 16, 16, 192
HEADS = 12
KD = C // HEADS
WS = 14
MLP = 768
EPS = 1e-6
NIMG = H * W
T = B * NIMG
P = 128
NT = T // P
CHUNK = 512
NCH = T // CHUNK

WIN = WS * WS
HALF = WIN // 2
SIDE = WS * (W - WS)
REST = NIMG - WIN
MAIN = B * WIN
PAIR = 2 * REST
NP = B // 2
PADS = T
KCOLS = T + WIN

R_BIAS = 3 * KD
R_MASK = R_BIAS + 4 * WS
R_MAX = R_MASK + 6
ROWS = R_MAX + 2
R_CONST = 32
Q_CONST = 96
MASKED = -1.0e30

A8 = 8
VD = KD + 1
RING = 3


def natural(ap, img0, n):
    return ap[:, img0 * NIMG:(img0 + n) * NIMG].rearrange("p (i h w) -> p i h w", i=n, h=H)


def rest(ap):
    return ap[:, MAIN:T].rearrange("p (i t) -> p i t", i=B)


def window_attention_block(nc, x, qkv_w, proj_w, mlp_w1, mlp_w2, vectors, rows, rel, kconst, qconst, ident_in, out):
    x_tiles = x.rearrange("b h w c -> (b h w) c").rearrange("(t p) c -> p t c", p=P)
    out_tiles = out.rearrange("b h w c -> (b h w) c").rearrange("(t p) c -> p t c", p=P)

    with ExitStack() as ctx:
        base = -(-nc.sbuf_base // 32) * 32

        def room(at, *tensors):
            placed = []
            for name, shape, *dt in tensors:
                placed.append(nc.alloc_sbuf_tensor_at(name, shape, dt[0] if dt else F32, offset=at))
                n = 4
                for k in shape[1:]:
                    n *= k
                at += -(-n // 32) * 32
            assert at <= nc.sbuf_usable_end, (at, nc.sbuf_usable_end)
            return at, placed

        def sem(name):
            return ctx.enter_context(nc.semaphore(name))

        ps = ctx.enter_context(nc.psum_tensor("ps", [P, 8, 512], F32))

        end, (ident, vec, vbias, bs, stats, mv, var, std, rstd, nmr, nmax, nmax_rest, shift, shift_rest,
              v_main, v_rest, v_pad, qop0, qop1, kop0, kop1) = room(
            base, ("ident", [P, P]), ("vec", [P, 32]), ("vbias", [P, C]), ("bs", [P, 3]), ("stats", [P, NT, 6]),
            ("mv", [P, NT, 2]), ("var", [P, NT]), ("std", [P, NT]), ("rstd", [P, NT]), ("nmr", [P, NT]),
            ("nmax", [HALF, 2, 2 * B]), ("nmax_rest", [PAIR, 2, NP]), ("shift", [2 * B, 2, 2, HALF]),
            ("shift_rest", [NP, 2, 2, PAIR]), ("v_main", [HALF, 2 * B, HEADS, VD]), ("v_rest", [PAIR, NP, HEADS, VD]),
            ("v_pad", [HALF, HEADS, VD]), ("qop0", [ROWS, T], F32R), ("qop1", [ROWS, T], F32R),
            ("kop0", [ROWS, KCOLS], F32R), ("kop1", [ROWS, KCOLS], F32R))
        split, (hi0, hi1, hi2, lo0, lo1, lo2, bh0, bh1, bh2, bl0, bl1, bl2) = room(
            end, ("hi0", [P, T]), ("hi1", [P, KCOLS]), ("hi2", [P, KCOLS]), ("lo0", [P, T]), ("lo1", [P, KCOLS]),
            ("lo2", [P, KCOLS]), ("bhi0", [P, T]), ("bhi1", [P, T]), ("bhi2", [P, T]), ("blo0", [P, T]),
            ("blo1", [P, T]), ("blo2", [P, T]))
        hi, lo, bhi, blo = (hi0, hi1, hi2), (lo0, lo1, lo2), (bh0, bh1, bh2), (bl0, bl1, bl2)
        _, (kst, qst) = room(end, ("kst", [ROWS, 512]), ("qst", [ROWS, T]))
        late, (xres, xn2, h20, h21, gl, w10, w11, w2t, wp0, wp1, on0, rb, sel) = room(
            end, ("xres", [P, NT, C]), ("xn2", [P, NT, C]), ("h20", [P, T]), ("h21", [C - P, T]),
            ("gl", [P, 2, 6, CHUNK]), ("w10", [P, MLP]), ("w11", [C - P, MLP]), ("w2t", [P, 6, C]), ("wp0", [P, C]),
            ("wp1", [C - P, C]), ("on0", [P, T]), ("rb", [P, 2, C]), ("sel", [P, C]))
        assert late <= split
        _, (xt, ht0, ht1, xf0, xf2, xf1, wq0, wq1, relc, reld8, reld4) = room(
            split, ("xt", [P, 2, 4, C]), ("ht0", [P, T]), ("ht1", [C - P, T]), ("xf0", [P, T]), ("xf2", [P, T]),
            ("xf1", [P, 2, CHUNK]), ("wq0", [P, 3 * C]), ("wq1", [C - P, 3 * C]), ("relc", [P, 2, 2 * WS - 1]),
            ("reld8", [P, 2, 2 * WS - 1, A8]), ("reld4", [P, 2, 2 * WS - 1, HEADS - A8]))
        htw = (bh0, bh1)
        _, (qop2, kop2, pm, ppad, prest, osb, ot0, ot1) = room(
            split, ("qop2", [ROWS, T], F32R), ("kop2", [ROWS, KCOLS], F32R), ("pm", [HALF, 2, 2, 2 * WIN]),
            ("ppad", [HALF, 2, B * REST]), ("prest", [PAIR, B * REST]), ("osb", [P, 2, 2 * WIN + PAIR]),
            ("ot0", [P, T]), ("ot1", [P, T]))
        _, (on1,) = room(split, ("on1", [C - P, T]))
        qop, kop = (qop0, qop1, qop2), (kop0, kop1, kop2)

        s = {n: sem(n) for n in (
            "w_in", "rel_in", "rel_zero", "x0_in", "x1_in", "x2_in", "x3_in", "kst_in", "qst_in", "ops_const", "bs_ready", "v_ones",
            "var_ready", "std_ready", "rstd_ready", "xn_ready", "tp_done", "ht0_ready", "ht1_ready",
            "proj_done", "xf_ready", "hi_ready", "lo_ready", "bias_done", "bhi_ready", "blo_ready",
            "v_done", "v_ready", "op_in", "op_in1", "op_in2", "s_done", "max_ready", "mt_done", "shift_ready", "shift_in", "shift_in1",
            "st_done", "exp_done", "pv_done", "osb_ready", "o_in", "o_in1", "psum_zero",
            "late_in", "rden_ready", "bc_done", "on_ready", "pr_done", "x2_ready", "st2_var", "st2_std", "st2_rstd", "xn2_ready",
            "tp2_done", "h20_ready", "h21_ready", "m1_done", "gl_ready", "m2_done", "y_ready", "y_out", "chain_dve", "chain_pool", "xpb_ready", "xb2_ready", "pads_ready", "reld_ready", "htw_ready",
        )}
        op_in = [s["op_in"], s["op_in1"], s["op_in2"]]
        shift_in = [s["shift_in"], s["shift_in1"]]
        o_in = [s["o_in"], s["o_in1"]]
        x_in = [s["x0_in"], s["x1_in"], s["x2_in"], s["x3_in"]]

        G1A, B1A, G1B, B1B, G2A, B2A, G2B, B2B = range(8)
        BQKV = 8
        BM1 = 11
        SCL = 17

        def place(h):
            if h < A8:
                return (0, KD * h), (1, KD * h), (0, h, A8), (1, h, A8)
            j = h - A8
            return (2, KD * j), (2, 64 + KD * j), (2, j, HEADS - A8), (2, 64 + j, HEADS - A8)

        N_OP = 10 * 16

        block = ctx.enter_context(nc.Block())

        @block.sync
        def _(sp):
            def load_x(c):
                sp.dma_start(xt[:, c % 2], x_tiles[:, 4 * c:4 * c + 4, :]).then_inc(x_in[c], 16)

            load_x(0)
            sp.dma_start(ident[:], ident_in).then_inc(s["w_in"], 16)
            sp.dma_start(vec[:], vectors).then_inc(s["w_in"], 16)
            load_x(1)
            for wt, r0, r1 in ((wq0, 0, P), (wq1, P, C)):
                for d0, s0, n in ((0, 0, P), (P, C, P), (2 * P, P, C - P), (2 * P + C - P, C + P, 2 * C - P)):
                    sp.dma_start(wt[:, d0:d0 + n], qkv_w[r0:r1, s0:s0 + n]).then_inc(s["w_in"], 16)
            sp.dma_start(vbias[:], rows[0:1, :].to_broadcast([P, C])).then_inc(s["w_in"], 16)
            sp.dma_start(kst[R_CONST:ROWS, :], kconst).then_inc(s["kst_in"], 16)
            sp.dma_start(qst[Q_CONST:ROWS, :], qconst).then_inc(s["qst_in"], 16)
            for j in range(A8):
                sp.dma_start(relc[KD * j:KD * (j + 1)], rel).then_inc(s["rel_in"], 16)
            for c in range(2, NCH):
                sp.wait_ge(s["tp_done"], 2 * (c - 1))
                load_x(c)

            def load_operands(h):
                (tq, rq), (tk, rk), (tr, rr, sr), (tw, rw, sw) = place(h)
                q, k, sl = qop[h % RING], kop[h % RING], op_in[h % RING]
                if h >= RING:
                    sp.wait_ge(s["st_done"], 6 * (h - RING + 1))
                if h == 0:
                    sp.wait_ge(s["ops_const"], 2)
                    sp.wait_ge(s["lo_ready"], 12)
                    sp.wait_ge(s["pads_ready"], 4)
                    sp.wait_ge(s["bhi_ready"], 8)
                    sp.wait_ge(s["blo_ready"], 8)
                if h == A8 or h == 2:
                    sp.wait_ge(s["bhi_ready"], 16)
                    sp.wait_ge(s["blo_ready"], 16)
                if h >= 1:
                    sp.wait_ge(s["ops_const"], 3)
                for dst, src, r0, st, n in ((0, hi[tq], rq, 1, KD), (KD, lo[tq], rq, 1, KD), (2 * KD, hi[tq], rq, 1, KD),
                                            (R_BIAS, bhi[tr], rr, sr, WS), (R_BIAS + WS, bhi[tw], rw, sw, WS),
                                            (R_BIAS + 2 * WS, blo[tr], rr, sr, WS), (R_BIAS + 3 * WS, blo[tw], rw, sw, WS)):
                    sp.dma_start(q[dst:dst + n, 0:T].bitcast(F32), src[r0:r0 + st * (n - 1) + 1:st, 0:T]).then_inc(sl, 16)
                for dst, src in ((0, hi[tk]), (KD, hi[tk]), (2 * KD, lo[tk])):
                    sp.dma_start(k[dst:dst + KD, :].bitcast(F32), src[rk:rk + KD, :]).then_inc(sl, 16)

            def load_shift(h):
                q = qop[h % RING]
                sp.wait_ge(s["shift_ready"], 4 * (h + 1))
                for part in range(2):
                    row = R_MAX + part
                    sp.dma_start(q[row:row + 1, 0:MAIN].bitcast(F32).rearrange("o (g t) -> o g t", t=HALF),
                                 shift[:, h % 2, part, :]).then_inc(shift_in[h % 2], 16)
                    sp.dma_start(q[row:row + 1, MAIN:T].bitcast(F32).rearrange("o (g t) -> o g t", t=PAIR),
                                 shift_rest[:, h % 2, part, :]).then_inc(shift_in[h % 2], 16)

            def store_heads_output(h):
                sp.wait_ge(s["osb_ready"], 2 * (h + 1))
                o, dst, r0 = osb[:, h % 2], (ot0 if h < A8 else ot1), KD * (h % A8)
                for j in range(4):
                    sp.dma_start(dst[r0:r0 + KD, 0:MAIN].rearrange("c (g i t) -> c g i t", g=2, i=4)[:, :, j],
                                 o[32 * j:32 * j + KD, 0:2 * WIN].rearrange("c (g t) -> c g t", g=2)).then_inc(o_in[h % 2], 16)
                    sp.dma_start(dst[r0:r0 + KD, MAIN + PAIR * j:MAIN + PAIR * (j + 1)],
                                 o[32 * j:32 * j + KD, 2 * WIN:2 * WIN + PAIR]).then_inc(o_in[h % 2], 16)
                    den = ot1[64 + h:65 + h]
                    sp.dma_start(den[:, 0:MAIN].rearrange("c (g i t) -> c g i t", g=2, i=4)[:, :, j],
                                 o[32 * j + KD:32 * j + VD, 0:2 * WIN].rearrange("c (g t) -> c g t", g=2)).then_inc(o_in[h % 2], 16)
                    sp.dma_start(den[:, MAIN + PAIR * j:MAIN + PAIR * (j + 1)],
                                 o[32 * j + KD:32 * j + VD, 2 * WIN:2 * WIN + PAIR]).then_inc(o_in[h % 2], 16)

            load_operands(0)
            load_operands(1)
            load_shift(0)
            for h in range(HEADS):
                if h + 2 < HEADS:
                    load_operands(h + 2)
                if h + 1 < HEADS:
                    load_shift(h + 1)
                store_heads_output(h)
                if h == HEADS - 2:
                    for r in range(RING):
                        sp.wait_ge(op_in[r], N_OP * (HEADS // RING))
                    for t in range(0, NT, 4):
                        sp.dma_start(xres[:, t:t + 4], x_tiles[:, t:t + 4]).then_inc(s["late_in"], 16)
                    for dst, src in ((w10[:], mlp_w1[0:P]), (w11[:], mlp_w1[P:C]),
                                     (w2t[:], mlp_w2.rearrange("(m p) c -> p m c", p=P)),
                                     (wp0[:], proj_w[0:P]), (wp1[:], proj_w[P:C]),
                                     (rb[:, 0], rows[1:2, :].to_broadcast([P, C])),
                                     (rb[:, 1], rows[2:3, :].to_broadcast([P, C])),
                                     (sel[64:64 + HEADS, :], rows[3:3 + HEADS, :])):
                        sp.dma_start(dst, src).then_inc(s["late_in"], 16)
            for t in range(0, NT, 2):
                sp.wait_ge(s["y_ready"], t // 2 + 1)
                sp.dma_start(out_tiles[:, t:t + 2], xn2[:, t:t + 2]).then_inc(s["y_out"], 16)
            sp.wait_ge(s["y_out"], 16 * (NT // 2))

        @block.gpsimd
        def _(pool):
            g = nc.gpsimd
            n_chain = [0]

            def after(ins):
                n_chain[0] += 1
                ins.then_inc(s["chain_pool"], 1)
                pool.wait_ge(s["chain_pool"], n_chain[0])


            def key_consts(k):
                for r0, r1 in ((R_CONST, 64), (64, ROWS)):
                    src = kst[r0:r1]
                    g.tensor_copy(k[r0:r1, 0:MAIN].rearrange("p (i t) -> p i t", i=B),
                                  src[:, 0:WIN].unsqueeze(1).to_broadcast([r1 - r0, B, WIN]))
                    g.tensor_copy(k[r0:r1, MAIN:T].rearrange("p (i t) -> p i t", i=NP),
                                  src[:, WIN:WIN + PAIR].unsqueeze(1).to_broadcast([r1 - r0, NP, PAIR]))
                    after(g.tensor_copy(k[r0:r1, PADS:KCOLS], src[:, WIN + PAIR:2 * WIN + PAIR]))

            def normalise(c):
                pool.wait_ge(x_in[c], 16)
                pool.wait_ge(s["rstd_ready"], c + 1)
                for k in range(4):
                    t = 4 * c + k
                    g.tensor_scalar(xt[:, c % 2, k], xt[:, c % 2, k], rstd[:, t:t + 1], nmr[:, t:t + 1],
                                    ALU.mult, ALU.add).then_inc(s["xn_ready"], 1)

            normalise(0)
            pool.wait_ge(s["xn_ready"], 4)
            pool.wait_ge(s["kst_in"], 16)
            pool.wait_ge(s["qst_in"], 16)
            for i in range(2):
                key_consts(kop[i])
                g.tensor_copy(qop[i][Q_CONST:ROWS, :], qst[Q_CONST:ROWS, :]).then_inc(s["ops_const"], 1)
                pool.wait_ge(s["ops_const"], i + 1)

            def split_hi(m, c):
                u = 3 * c + m
                pool.wait_ge(s["xf_ready"], u + 1)
                if u == 0:
                    pool.wait_ge(s["ops_const"], 2)
                src = natural((xf0, None, xf2)[m], 2 * c, 2) if m != 1 else \
                    xf1[:, c % 2].rearrange("p (i h w) -> p i h w", i=2, h=H)
                main = hi[m][:, 2 * c * WIN:2 * (c + 1) * WIN].rearrange("p (i h w) -> p i h w", i=2, h=WS)
                r = rest(hi[m])[:, 2 * c:2 * c + 2]
                g.tensor_copy(main.bitcast(F32R), src[:, :, 0:WS, 0:WS])
                g.tensor_copy(r[:, :, 0:SIDE].rearrange("p i (h w) -> p i h w", h=WS).bitcast(F32R), src[:, :, 0:WS, WS:W])
                g.tensor_copy(r[:, :, SIDE:REST].rearrange("p i (h w) -> p i h w", w=W).bitcast(F32R),
                              src[:, :, WS:H, :]).then_inc(s["hi_ready"], 1)

            def pads(m, n):
                bias = bs[:, m:m + 1].to_broadcast([P, WIN])
                g.tensor_copy(hi[m][:, PADS:KCOLS].bitcast(F32R), bias).then_inc(s["pads_ready"], 1)
                pool.wait_ge(s["pads_ready"], 2 * n + 1)
                g.tensor_tensor(lo[m][:, PADS:KCOLS].bitcast(F32R), bias, hi[m][:, PADS:KCOLS],
                                ALU.subtract).then_inc(s["pads_ready"], 1)

            def window_order(c):
                for kc, (ht, ready, r) in enumerate(((ht0, "ht0_ready", P), (ht1, "ht1_ready", C - P))):
                    pool.wait_ge(s[ready], c + 1)
                    if kc:
                        pool.wait_ge(s["htw_ready"], 2 * c + 1)
                    src, rs = natural(ht, 2 * c, 2), rest(htw[kc])[0:r, 2 * c:2 * c + 2]
                    g.tensor_copy(htw[kc][0:r, 2 * c * WIN:2 * (c + 1) * WIN].rearrange("p (i h w) -> p i h w", i=2, h=WS),
                                  src[:, :, 0:WS, 0:WS])
                    g.tensor_copy(rs[:, :, 0:SIDE].rearrange("p i (h w) -> p i h w", h=WS), src[:, :, 0:WS, WS:W])
                    g.tensor_copy(rs[:, :, SIDE:REST].rearrange("p i (h w) -> p i h w", w=W),
                                  src[:, :, WS:H, :]).then_inc(s["htw_ready"], 1)
                pool.wait_ge(s["htw_ready"], 2 * c + 2)

            for c in range(1, NCH):
                normalise(c)
                window_order(c - 1)
                for m in range(3):
                    split_hi(m, c - 1)
            window_order(NCH - 1)
            for m in range(3):
                split_hi(m, NCH - 1)
            pool.wait_ge(s["rel_in"], 16 * A8)
            for d, nh in ((reld8, A8), (reld4, HEADS - A8)):
                g.tensor_tensor(d[:].rearrange("p a r j -> p (a r) j"),
                                relc[:].rearrange("p a r -> p (a r)").unsqueeze(2).to_broadcast([P, 2 * (2 * WS - 1), nh]),
                                vec[:, 24:24 + nh].unsqueeze(1).to_broadcast([P, 2 * (2 * WS - 1), nh]),
                                ALU.mult).then_inc(s["reld_ready"], 1)
            pool.wait_ge(s["bs_ready"], 1)
            pads(1, 0)
            pads(2, 1)
            pool.wait_ge(s["pads_ready"], 4)
            pool.wait_ge(s["bias_done"], 16)
            pool.wait_ge(s["v_done"], 10)
            pool.wait_ge(s["lo_ready"], 12)
            for r0, r1 in ((R_CONST, 64), (64, ROWS)):
                after(g.tensor_copy(kop[2][r0:r1, :], kop[1][r0:r1, :].bitcast(F32)))
            g.tensor_copy(qop[2][Q_CONST:ROWS, :], qop[1][Q_CONST:ROWS, :].bitcast(F32)).then_inc(s["ops_const"], 1)

            pool.wait_ge(s["ops_const"], 3)
            pool.wait_ge(s["late_in"], 12 * 16)
            for c in range(NCH):
                g.tensor_tensor(xres[:, 4 * c:4 * c + 4], xres[:, 4 * c:4 * c + 4],
                                rb[:, 0:1].to_broadcast([P, 4, C]), ALU.add).then_inc(s["xpb_ready"], 1)
            for t in range(NT):
                if t == 0:
                    pool.wait_ge(s["st2_rstd"], 1)
                g.tensor_scalar(xn2[:, t], xres[:, t], rstd[:, t:t + 1], nmr[:, t:t + 1],
                                ALU.mult, ALU.add).then_inc(s["xn2_ready"], 1)
                if t % 4 == 3:
                    c = t // 4
                    pool.wait_ge(s["xn2_ready"], t + 1)
                    g.tensor_tensor(xres[:, 4 * c:4 * c + 4], xres[:, 4 * c:4 * c + 4],
                                    rb[:, 1:2].to_broadcast([P, 4, C]), ALU.add).then_inc(s["xb2_ready"], 1)

        @block.scalar
        def _(act):
            a = nc.scalar

            def std_of(c):
                act.wait_ge(s["var_ready"], c + 1)
                a.activation(std[:, 4 * c:4 * c + 4], var[:, 4 * c:4 * c + 4], ACT.Sqrt).then_inc(s["std_ready"], 1)

            def channels0(c):
                act.wait_ge(s["tp_done"], 2 * c + 1)
                a.activation(ht0[:, c * CHUNK:(c + 1) * CHUNK], ps[:, c % 2, :], ACT.Identity,
                             scale=vec[:, G1A:G1A + 1], bias=vec[:, B1A:B1A + 1]).then_inc(s["ht0_ready"], 1)

            def unit(m, c):
                u = 3 * c + m
                act.wait_ge(s["proj_done"], u + 1)
                if m == 1 and c >= 2:
                    act.wait_ge(s["lo_ready"], 3 * (c - 2) + 2)
                    act.wait_ge(s["hi_ready"], 3 * (c - 2) + 2)
                dst = xf1[:, c % 2] if m == 1 else (xf0, None, xf2)[m][:, c * CHUNK:(c + 1) * CHUNK]
                a.activation(dst, ps[:, 4 + u % 4, :], ACT.Identity, scale=vec[:, SCL + m:SCL + m + 1],
                             bias=bs[:, m:m + 1]).then_inc(s["xf_ready"], 1)

            act.wait_ge(s["w_in"], 11 * 16)
            std_of(0)
            std_of(1)
            act.wait_ge(s["bs_ready"], 1)
            for c in range(NCH):
                channels0(c)
                if c + 2 < NCH:
                    std_of(c + 2)
                for m in range(3):
                    unit(m, c)

            def bias_parts(v, out_main, out_side, out_low, fn):
                kind, b = v // 4, v % 4
                r0, r1 = (0, 112) if kind < 2 else ((0, 56) if kind == 2 else (64, 120))
                bank = ps[r0:r1, 4 + v % 4, :].rearrange("p (j i t) -> p j i t", j=4, i=B)
                tile_ = min(kind, 2)
                main = out_main[tile_][r0:r1, 0:MAIN].rearrange("p (i h w) -> p h i w", i=B, h=WS)
                mainw = out_main[tile_][r0:r1, 0:MAIN].rearrange("p (i h w) -> p w i h", i=B, h=WS)
                rst = rest(out_main[tile_])[r0:r1]
                side = rst[:, :, 0:SIDE].rearrange("p i (h w) -> p h i w", h=WS)
                sidew = rst[:, :, 0:SIDE].rearrange("p i (h w) -> p w i h", h=WS)
                low = rst[:, :, SIDE:REST].rearrange("p i (h w) -> p h i w", w=W)
                loww = rst[:, :, SIDE:REST].rearrange("p i (h w) -> p w i h", w=W)
                j0, j1 = 4 * b, min(4 * b + 4, WS)
                n = j1 - j0
                last = None
                if kind in (0, 2):
                    fn(main[:, j0:j1], bank[:, 0:n, :, 0:WS])
                    last = fn(side[:, j0:j1], bank[:, 0:n, :, WS:W])
                    if b == 3:
                        last = fn(low[:, 0:2], bank[:, 2:4, :, :])
                else:
                    fn(mainw[:, j0:j1], bank[:, 0:n, :, 0:WS])
                    last = fn(loww[:, 4 * b:4 * b + 4], bank[:, :, :, WS:H])
                    if b == 3:
                        last = fn(sidew[:, 0:2], bank[:, 2:4, :, 0:WS])
                return last

            act.wait_ge(s["v_done"], 10)
            for v in range(16):
                act.wait_ge(s["bias_done"], v + 1)
                bias_parts(v, bhi, None, None,
                           lambda o, i: a.copy(o.bitcast(F32R), i)).then_inc(s["bhi_ready"], 1)

            def shifts(h):
                act.wait_ge(s["mt_done"], h + 1)
                if h >= 2:
                    act.wait_ge(shift_in[h % 2], 64 * (h // 2))
                a.copy(shift[:, h % 2, 0, :].bitcast(F32R), ps[0:2 * B, 0, 128:128 + HALF]).then_inc(s["shift_ready"], 1)
                a.copy(shift_rest[:, h % 2, 0, :].bitcast(F32R), ps[0:NP, 0, 256:256 + PAIR]).then_inc(s["shift_ready"], 1)

            def exp_group(h, gi):
                n = 6 * h + gi
                act.wait_ge(s["st_done"], n + 1)
                if h == 0 and gi == 0:
                    act.wait_ge(s["blo_ready"], 16)
                b0 = 2 + 2 * (n % 2)
                if gi < 4:
                    k = 4 * h + gi
                    if k >= 2:
                        act.wait_ge(s["pv_done"], 6 * ((k - 2) // 4) + (k - 2) % 4 + 1)
                    a.activation(pm[:, gi % 2], ps[0:HALF, b0:b0 + 2, 0:2 * WIN], ACT.Exp).then_inc(s["exp_done"], 1)
                elif gi == 4:
                    if h:
                        act.wait_ge(s["pv_done"], 6 * h)
                    a.activation(ppad[:], ps[0:HALF, b0:b0 + 2, 0:B * REST], ACT.Exp).then_inc(s["exp_done"], 1)
                else:
                    a.activation(prest[:], ps[0:PAIR, b0, 0:B * REST], ACT.Exp).then_inc(s["exp_done"], 1)

            def outputs(h):
                if h >= 2:
                    act.wait_ge(o_in[h % 2], 16 * 16 * (h // 2))
                act.wait_ge(s["pv_done"], 6 * h + 6)
                a.copy(osb[:, h % 2, 0:2 * WIN], ps[:, 6, 0:2 * WIN]).then_inc(s["osb_ready"], 1)
                a.copy(osb[:, h % 2, 2 * WIN:2 * WIN + PAIR], ps[:, 7, 0:PAIR]).then_inc(s["osb_ready"], 1)

            shifts(0)
            for h in range(HEADS):
                for gi in range(6):
                    if gi == 5 and h + 1 < HEADS:
                        shifts(h + 1)
                    exp_group(h, gi)
                outputs(h)

            act.wait_ge(s["st2_var"], 1)
            a.activation(std[:], var[:], ACT.Sqrt).then_inc(s["st2_std"], 1)
            for c in range(NCH):
                act.wait_ge(s["tp2_done"], 2 * c + 1)
                a.activation(h20[:, c * CHUNK:(c + 1) * CHUNK], ps[:, c % 2, :], ACT.Identity,
                             scale=vec[:, G2A:G2A + 1], bias=vec[:, B2A:B2A + 1]).then_inc(s["h20_ready"], 1)
                for m in range(6):
                    n = 6 * c + m
                    act.wait_ge(s["m1_done"], n + 1)
                    if c >= 2 and m == 0:
                        act.wait_ge(s["m2_done"], 2 * (c - 1))
                    a.activation(gl[:, c % 2, m], ps[:, 4 + n % 2, :], ACT.Gelu,
                                 bias=vec[:, BM1 + m:BM1 + m + 1]).then_inc(s["gl_ready"], 1)

        @block.vector
        def _(dve):
            v_ = nc.vector
            n_chain = [0]

            def after(ins):
                n_chain[0] += 1
                ins.then_inc(s["chain_dve"], 1)
                dve.wait_ge(s["chain_dve"], n_chain[0])

            def stats_of(src, tiles):
                for t in tiles:
                    o = v_.bn_stats(stats[:, t], src(t))
                after(o)
                for t in tiles:
                    o = v_.bn_aggr(mv[:, t], stats[:, t])
                after(o)

            def rstd_of(t0, t1):
                after(v_.reciprocal(rstd[:, t0:t1], std[:, t0:t1]))
                return v_.scalar_tensor_tensor(nmr[:, t0:t1], mv[:, t0:t1, 0], -1.0, rstd[:, t0:t1], ALU.mult, ALU.mult)

            v_.memset(v_pad[:, :, KD:VD], 1.0)
            v_.memset(v_main[:, :, :, KD:VD], 1.0)
            v_.memset(v_rest[:, :, :, KD:VD], 1.0)
            dve.wait_ge(s["w_in"], 11 * 16)
            v_.tensor_tensor(bs[:], vec[:, BQKV:BQKV + 3], vec[:, SCL:SCL + 3], ALU.mult).then_inc(s["bs_ready"], 1)
            v_.tensor_copy(v_pad[:, :, 0:KD], vbias[0:HALF].rearrange("p (h d) -> p h d", h=HEADS))

            def early_stats(c):
                dve.wait_ge(x_in[c], 16)
                stats_of(lambda t: xt[:, c % 2, t - 4 * c], range(4 * c, 4 * c + 4))
                v_.tensor_scalar(var[:, 4 * c:4 * c + 4], mv[:, 4 * c:4 * c + 4, 1], EPS, None,
                                 ALU.add).then_inc(s["var_ready"], 1)

            def early_rstd(c):
                dve.wait_ge(s["std_ready"], c + 1)
                rstd_of(4 * c, 4 * c + 4).then_inc(s["rstd_ready"], 1)

            def channels1(c):
                dve.wait_ge(s["tp_done"], 2 * c + 2)
                v_.tensor_scalar(ht1[:, c * CHUNK:(c + 1) * CHUNK], ps[0:64, 2 + c % 2, :], vec[0:64, G1B:G1B + 1],
                                 vec[0:64, B1B:B1B + 1], ALU.mult, ALU.add).then_inc(s["ht1_ready"], 1)

            def split_lo(m, c):
                u = 3 * c + m
                dve.wait_ge(s["hi_ready"], u + 1)
                dve.wait_ge(s["xf_ready"], u + 1)
                src = natural((xf0, None, xf2)[m], 2 * c, 2) if m != 1 else \
                    xf1[:, c % 2].rearrange("p (i h w) -> p i h w", i=2, h=H)

                def parts(tile_):
                    r = rest(tile_)[:, 2 * c:2 * c + 2]
                    return (tile_[:, 2 * c * WIN:2 * (c + 1) * WIN].rearrange("p (i h w) -> p i h w", i=2, h=WS),
                            r[:, :, 0:SIDE].rearrange("p i (h w) -> p i h w", h=WS),
                            r[:, :, SIDE:REST].rearrange("p i (h w) -> p i h w", w=W))
                views = (src[:, :, 0:WS, 0:WS], src[:, :, 0:WS, WS:W], src[:, :, WS:H, :])
                for o, i, h_ in zip(parts(lo[m]), views, parts(hi[m])):
                    ins = v_.tensor_tensor(o.bitcast(F32R), i, h_, ALU.subtract)
                ins.then_inc(s["lo_ready"], 1)

            early_stats(0)
            early_stats(1)
            early_rstd(0)
            for c in range(NCH):
                if c + 1 < NCH:
                    early_rstd(c + 1)
                channels1(c)
                if c + 2 < NCH:
                    early_stats(c + 2)
                if c:
                    for m in range(3):
                        split_lo(m, c - 1)
            for m in range(3):
                split_lo(m, NCH - 1)

            for u in range(10):
                dve.wait_ge(s["v_done"], u + 1)
                n = HALF if u < 8 else PAIR
                src = ps[0:n, u % 4, 0:2 * C].rearrange("p (k h d) -> p k h d", k=2, h=HEADS)
                dst = v_main[:, 2 * u:2 * u + 2] if u < 8 else v_rest[:, 2 * (u - 8):2 * (u - 8) + 2]
                for k in range(2):
                    o = v_.tensor_tensor(dst[:, k, :, 0:KD], src[:, k],
                                         vbias[0:n].rearrange("p (h d) -> p h d", h=HEADS), ALU.add)
                o.then_inc(s["v_ready"], 1)

            def bias_lo(v):
                kind, b = v // 4, v % 4
                dve.wait_ge(s["bhi_ready"], v + 1)
                r0, r1 = (0, 112) if kind < 2 else ((0, 56) if kind == 2 else (64, 120))
                bank = ps[r0:r1, 4 + v % 4, :].rearrange("p (j i t) -> p j i t", j=4, i=B)
                t_ = min(kind, 2)
                n = min(4, WS - 4 * b)

                def views(tile_):
                    m_ = tile_[r0:r1, 0:MAIN]
                    r_ = rest(tile_)[r0:r1]
                    if kind in (0, 2):
                        w = [m_.rearrange("p (i h w) -> p h i w", i=B, h=WS)[:, 4 * b:4 * b + n],
                             r_[:, :, 0:SIDE].rearrange("p i (h w) -> p h i w", h=WS)[:, 4 * b:4 * b + n]]
                        if b == 3:
                            w.append(r_[:, :, SIDE:REST].rearrange("p i (h w) -> p h i w", w=W)[:, 0:2])
                    else:
                        w = [m_.rearrange("p (i h w) -> p w i h", i=B, h=WS)[:, 4 * b:4 * b + n],
                             r_[:, :, SIDE:REST].rearrange("p i (h w) -> p w i h", w=W)[:, 4 * b:4 * b + 4]]
                        if b == 3:
                            w.append(r_[:, :, 0:SIDE].rearrange("p i (h w) -> p w i h", h=WS)[:, 0:2])
                    return w
                if kind in (0, 2):
                    srcs = [bank[:, 0:n, :, 0:WS], bank[:, 0:n, :, WS:W], bank[:, 2:4, :, :]]
                else:
                    srcs = [bank[:, 0:n, :, 0:WS], bank[:, :, :, WS:H], bank[:, 2:4, :, 0:WS]]
                for o, i, h_ in zip(views(blo[t_]), srcs, views(bhi[t_])):
                    ins = v_.tensor_tensor(o.bitcast(F32R), i, h_, ALU.subtract)
                ins.then_inc(s["blo_ready"], 1)

            for v in range(16):
                bias_lo(v)

            def maxima(h, n):
                k = 12 * h + n
                dve.wait_ge(s["s_done"], k + 1)
                if n == 0 and h >= 2:
                    dve.wait_ge(s["mt_done"], h - 1)
                if n < B:
                    v_.tensor_reduce(nmax[:, h % 2, 2 * n:2 * n + 2],
                                     ps[0:HALF, k % 2, 0:2 * WIN].rearrange("p (t k) -> p t k", t=2),
                                     AX.X, ALU.max, negate=True).then_inc(s["max_ready"], 1)
                else:
                    p_ = n - B
                    v_.tensor_reduce(nmax_rest[:, h % 2, p_:p_ + 1], ps[0:PAIR, k % 2, 0:PAIR + WIN],
                                     AX.X, ALU.max, negate=True).then_inc(s["max_ready"], 1)

            def shifts_lo(h):
                dve.wait_ge(s["shift_ready"], 4 * h + 2)
                v_.tensor_tensor(shift[:, h % 2, 1, :].bitcast(F32R), ps[0:2 * B, 0, 128:128 + HALF],
                                 shift[:, h % 2, 0, :], ALU.subtract).then_inc(s["shift_ready"], 1)
                v_.tensor_tensor(shift_rest[:, h % 2, 1, :].bitcast(F32R), ps[0:NP, 0, 256:256 + PAIR],
                                 shift_rest[:, h % 2, 0, :], ALU.subtract).then_inc(s["shift_ready"], 1)

            for h in range(HEADS):
                for n in range(12):
                    maxima(h, n)
                shifts_lo(h)

            for k in range(2):
                dve.wait_ge(o_in[k], 16 * 16 * HEADS // 2)
            v_.reciprocal(ot1[64:64 + HEADS, :], ot1[64:64 + HEADS, :]).then_inc(s["rden_ready"], 1)
            for u in range(5):
                dve.wait_ge(s["bc_done"], u + 1)
                for (o_, src, r, bk) in ((on0, ot0, P, 2 * (u % 2)), (on1, ot1, 64, 2 * (u % 2) + 1)):
                    if u < 4:
                        o = v_.tensor_tensor(
                            natural(o_, 2 * u, 2)[:, :, 0:WS, 0:WS],
                            src[0:r, 2 * u * WIN:2 * (u + 1) * WIN].rearrange("p (i h w) -> p i h w", i=2, h=WS),
                            ps[0:r, bk, 0:2 * WIN].rearrange("p (i h w) -> p i h w", i=2, h=WS), ALU.mult)
                    else:
                        rs = rest(src)[0:r]
                        bb = ps[0:r, bk, 0:B * REST].rearrange("p (i t) -> p i t", i=B)
                        v_.tensor_tensor(natural(o_, 0, B)[:, :, 0:WS, WS:W],
                                         rs[:, :, 0:SIDE].rearrange("p i (h w) -> p i h w", h=WS),
                                         bb[:, :, 0:SIDE].rearrange("p i (h w) -> p i h w", h=WS), ALU.mult)
                        o = v_.tensor_tensor(natural(o_, 0, B)[:, :, WS:H, :],
                                             rs[:, :, SIDE:REST].rearrange("p i (h w) -> p i h w", w=W),
                                             bb[:, :, SIDE:REST].rearrange("p i (h w) -> p i h w", w=W), ALU.mult)
                    o.then_inc(s["on_ready"], 1)

            for u in range(NT // 2):
                dve.wait_ge(s["pr_done"], u + 1)
                dve.wait_ge(s["xpb_ready"], u // 2 + 1)
                v_.tensor_tensor(xres[:, 2 * u:2 * u + 2], ps[:, 4 + u % 4, 0:2 * C].rearrange("p (k c) -> p k c", k=2),
                                 xres[:, 2 * u:2 * u + 2], ALU.add).then_inc(s["x2_ready"], 1)
                dve.wait_ge(s["x2_ready"], u + 1)
                for t in (2 * u, 2 * u + 1):
                    o = v_.bn_stats(stats[:, t], xres[:, t])
            after(o)
            for t in range(NT):
                o = v_.bn_aggr(mv[:, t], stats[:, t])
            after(o)
            v_.tensor_scalar(var[:], mv[:, :, 1], EPS, None, ALU.add).then_inc(s["st2_var"], 1)
            dve.wait_ge(s["st2_std"], 1)
            rstd_of(0, NT).then_inc(s["st2_rstd"], 1)

            def second_channels1(c):
                dve.wait_ge(s["tp2_done"], 2 * c + 2)
                v_.tensor_scalar(h21[:, c * CHUNK:(c + 1) * CHUNK], ps[0:64, 2 + c % 2, :], vec[0:64, G2B:G2B + 1],
                                 vec[0:64, B2B:B2B + 1], ALU.mult, ALU.add).then_inc(s["h21_ready"], 1)

            def results(c):
                for u in (2 * c, 2 * c + 1):
                    dve.wait_ge(s["m2_done"], u + 1)
                    dve.wait_ge(s["xb2_ready"], c + 1)
                    v_.tensor_tensor(xn2[:, 2 * u:2 * u + 2], ps[:, 6 + u % 2, 0:2 * C].rearrange("p (k c) -> p k c", k=2),
                                     xres[:, 2 * u:2 * u + 2], ALU.add).then_inc(s["y_ready"], 1)

            second_channels1(0)
            for c in range(NCH):
                if c + 1 < NCH:
                    second_channels1(c + 1)
                results(c)

        @block.tensor
        def _(pe):
            mm = nc.tensor.matmul

            pe.wait_ge(s["w_in"], 11 * 16)

            def transposes(c, src, ready, done, evac0, evac1):
                pe.wait_ge(ready, 4 * (c + 1))
                if c >= 2:
                    pe.wait_ge(evac0, c - 1)
                    pe.wait_ge(evac1, c - 1)
                for k in range(4):
                    o = nc.tensor.transpose(ps[:, c % 2, P * k:P * (k + 1)], src(c, k)[:, 0:P], ident[:])
                o.then_inc(done, 1)
                for k in range(4):
                    o = nc.tensor.transpose(ps[0:64, 2 + c % 2, P * k:P * (k + 1)], src(c, k)[:, P:C], ident[:])
                o.then_inc(done, 1)

            def project(c):
                cols = slice(c * CHUNK, (c + 1) * CHUNK)
                pe.wait_ge(s["ht0_ready"], c + 1)
                pe.wait_ge(s["ht1_ready"], c + 1)
                for m in range(3):
                    u = 3 * c + m
                    if u >= 4:
                        pe.wait_ge(s["xf_ready"], u - 3)
                    for k, (wt, ht) in enumerate(((wq0, ht0), (wq1, ht1))):
                        o = mm(ps[:, 4 + u % 4, :], wt[:, P * m:P * (m + 1)], ht[:, cols], start=(k == 0), stop=(k == 1))
                    o.then_inc(s["proj_done"], 1)

            def early_src(c, k):
                return xt[:, c % 2, k]

            for c in range(NCH):
                transposes(c, early_src, s["xn_ready"], s["tp_done"], s["ht0_ready"], s["ht1_ready"])
                if c:
                    project(c - 1)
            project(NCH - 1)

            for u in range(10):
                if u < 4:
                    pe.wait_ge(s["ht0_ready"], NCH)
                    pe.wait_ge(s["ht1_ready"], NCH)
                if u == 0:
                    pe.wait_ge(s["htw_ready"], 2 * NCH)
                if u >= 4:
                    pe.wait_ge(s["v_ready"], u - 3)
                for k in range(2):
                    n, c0 = (HALF, HALF * (2 * u + k)) if u < 8 else (PAIR, MAIN + PAIR * (2 * (u - 8) + k))
                    for kc, (wt, r) in enumerate(((wq0, P), (wq1, C - P))):
                        o = mm(ps[0:n, u % 4, C * k:C * (k + 1)], htw[kc][0:r, c0:c0 + n], wt[:, 2 * C:3 * C],
                               start=(kc == 0), stop=(kc == 1))
                o.then_inc(s["v_done"], 1)

            pe.wait_ge(s["reld_ready"], 2)
            pe.wait_ge(s["xf_ready"], 12)
            for v in range(16):
                kind, b = v // 4, v % 4
                if v >= 4:
                    pe.wait_ge(s["blo_ready"], v - 3)
                table, nh = (reld8, A8) if kind < 2 else (reld4, HEADS - A8)
                table = table[:, kind % 2].rearrange("p r j -> p (r j)")
                part = slice(0, 112) if kind < 2 else slice(0, 56) if kind == 2 else slice(64, 120)
                src = natural(xf0 if kind < 2 else xf2, 0, B)
                for j in range(4):
                    idx = 4 * b + j
                    shift0 = WS - 1 - idx % WS
                    r = src[:, :, idx, :] if kind in (0, 2) else src[:, :, :, idx]
                    o = mm(ps[part, 4 + v % 4, P * j:P * (j + 1)], table[:, shift0 * nh:(shift0 + WS) * nh], r,
                           start=True, stop=True)
                o.then_inc(s["bias_done"], 1)

            def score_piece(h, n):
                k = 12 * h + n
                q, kk, bank = qop[h % RING], kop[h % RING], k % 2
                if n == 0:
                    pe.wait_ge(op_in[h % RING], N_OP * (h // RING + 1))
                    if h == 0:
                        pe.wait_ge(s["v_ready"], 10)
                    else:
                        pe.wait_ge(s["shift_ready"], 4 * h)
                if k >= 2:
                    pe.wait_ge(s["max_ready"], k - 1)
                if n < B:
                    for t in range(2):
                        o = mm(ps[0:HALF, bank, WIN * t:WIN * (t + 1)],
                               q[0:R_MASK, WIN * n + HALF * t:WIN * n + HALF * (t + 1)],
                               kk[0:R_MASK, WIN * n:WIN * (n + 1)], start=True, stop=True)
                else:
                    c0 = MAIN + PAIR * (n - B)
                    mm(ps[0:PAIR, bank, 0:PAIR], q[0:R_MAX, c0:c0 + PAIR], kk[0:R_MAX, c0:c0 + PAIR], start=True, stop=True)
                    o = mm(ps[0:PAIR, bank, PAIR:PAIR + WIN], q[0:R_MAX, c0:c0 + PAIR], kk[0:R_MAX, PADS:KCOLS],
                           start=True, stop=True)
                o.then_inc(s["s_done"], 1)

            def max_rows(h):
                pe.wait_ge(s["max_ready"], 12 * (h + 1))
                nc.tensor.transpose(ps[0:2 * B, 0, 128:128 + HALF], nmax[:, h % 2, :], ident[0:HALF, 0:HALF])
                nc.tensor.transpose(ps[0:NP, 0, 256:256 + PAIR], nmax_rest[:, h % 2, :],
                                    ident[0:PAIR, 0:PAIR]).then_inc(s["mt_done"], 1)

            def weights(h, gi):
                n = 6 * h + gi
                q, kk, b0 = qop[h % RING], kop[h % RING], 2 + 2 * (n % 2)
                if gi == 0:
                    pe.wait_ge(shift_in[h % 2], 64 * (h // 2 + 1))
                if n >= 2:
                    pe.wait_ge(s["exp_done"], n - 1)
                if h == 0 and gi < 2:
                    pe.wait_ge(s["blo_ready"], 16)
                if gi < 4:
                    for i in range(2):
                        img = 2 * gi + i
                        for t in range(2):
                            o = mm(ps[0:HALF, b0 + i, WIN * t:WIN * (t + 1)],
                                   kk[:, WIN * img + HALF * t:WIN * img + HALF * (t + 1)],
                                   q[:, WIN * img:WIN * (img + 1)], start=True, stop=True)
                elif gi == 4:
                    for t in range(2):
                        o = mm(ps[0:HALF, b0 + t, 0:B * REST], kk[:, PADS + HALF * t:PADS + HALF * (t + 1)],
                               q[:, MAIN:T], start=True, stop=True)
                else:
                    for p_ in range(NP):
                        c0 = MAIN + PAIR * p_
                        o = mm(ps[0:PAIR, b0, PAIR * p_:PAIR * (p_ + 1)], kk[:, c0:c0 + PAIR], q[:, c0:c0 + PAIR],
                               start=True, stop=True)
                o.then_inc(s["st_done"], 1)

            def sums(h, gi):
                pe.wait_ge(s["exp_done"], 6 * h + gi + 1)
                if gi == 0 and h:
                    pe.wait_ge(s["osb_ready"], 2 * h - 1)
                if gi == 4 and h:
                    pe.wait_ge(s["osb_ready"], 2 * h)
                if gi < 4:
                    for t in range(2):
                        for i in range(2):
                            img = 2 * gi + i
                            r0, c0 = 32 * (img % 4), WIN * (img // 4)
                            o = mm(ps[r0:r0 + VD, 6, c0:c0 + WIN], v_main[:, 2 * img + t, h, :],
                                   pm[:, gi % 2, i, WIN * t:WIN * (t + 1)], start=(t == 0), stop=(t == 1))
                elif gi == 4:
                    for t in range(2):
                        for p_ in range(NP):
                            o = mm(ps[32 * p_:32 * p_ + VD, 7, 0:PAIR], v_pad[:, h, :],
                                   ppad[:, t, PAIR * p_:PAIR * (p_ + 1)], start=(t == 0), stop=False)
                else:
                    for p_ in range(NP):
                        o = mm(ps[32 * p_:32 * p_ + VD, 7, 0:PAIR], v_rest[:, p_, h, :],
                               prest[:, PAIR * p_:PAIR * (p_ + 1)], start=False, stop=True)
                o.then_inc(s["pv_done"], 1)

            plan = {0: (0, 1, 2), 1: (3, 4, 5), 2: (6, 7, 8, 9), 3: (10, 11)}
            for n in range(12):
                score_piece(0, n)
            max_rows(0)
            for h in range(HEADS):
                for gi in range(6):
                    weights(h, gi)
                    if h + 1 < HEADS:
                        for n in plan.get(gi, ()):
                            score_piece(h + 1, n)
                        if gi == 4:
                            max_rows(h + 1)
                    if gi:
                        sums(h, gi - 1)
                sums(h, 5)

            pe.wait_ge(s["rden_ready"], 1)
            pe.wait_ge(s["late_in"], 12 * 16)
            pe.wait_ge(s["exp_done"], 6 * HEADS)
            for u in range(5):
                c0, n = (2 * WIN * u, 2 * WIN) if u < 4 else (MAIN, B * REST)
                if u >= 2:
                    pe.wait_ge(s["on_ready"], 2 * (u - 1))
                mm(ps[:, 2 * (u % 2), 0:n], sel[64:64 + HEADS, 0:P], ot1[64:64 + HEADS, c0:c0 + n], start=True, stop=True)
                mm(ps[0:64, 2 * (u % 2) + 1, 0:n], sel[64:64 + HEADS, P:C], ot1[64:64 + HEADS, c0:c0 + n],
                   start=True, stop=True).then_inc(s["bc_done"], 1)
            pe.wait_ge(s["on_ready"], 10)
            pe.wait_ge(s["osb_ready"], 2 * HEADS)
            for u in range(NT // 2):
                if u >= 4:
                    pe.wait_ge(s["x2_ready"], u - 3)
                for k in range(2):
                    t = 2 * u + k
                    for kc, (o_, w_) in enumerate(((on0, wp0), (on1, wp1))):
                        o = mm(ps[:, 4 + u % 4, C * k:C * (k + 1)], o_[:, P * t:P * (t + 1)], w_[:],
                               start=(kc == 0), stop=(kc == 1))
                o.then_inc(s["pr_done"], 1)

            def late_src(c, k):
                return xn2[:, 4 * c + k]

            def second_transposes(c):
                transposes(c, late_src, s["xn2_ready"], s["tp2_done"], s["h20_ready"], s["h21_ready"])

            second_transposes(0)
            pe.wait_ge(s["x2_ready"], NT // 2)

            def hidden(c):
                pe.wait_ge(s["h20_ready"], c + 1)
                pe.wait_ge(s["h21_ready"], c + 1)
                for m in range(6):
                    n = 6 * c + m
                    if n >= 2:
                        pe.wait_ge(s["gl_ready"], n - 1)
                    for kc, (wt, ht) in enumerate(((w10, h20), (w11, h21))):
                        o = mm(ps[:, 4 + n % 2, :], wt[:, P * m:P * (m + 1)], ht[:, c * CHUNK:(c + 1) * CHUNK],
                               start=(kc == 0), stop=(kc == 1))
                    o.then_inc(s["m1_done"], 1)

            def second_layer(c):
                pe.wait_ge(s["gl_ready"], 6 * (c + 1))
                for u in (2 * c, 2 * c + 1):
                    if u >= 2:
                        pe.wait_ge(s["y_ready"], u - 1)
                    for k in range(2):
                        t = 2 * (u % 2) + k
                        for m in range(6):
                            o = mm(ps[:, 6 + u % 2, C * k:C * (k + 1)], gl[:, c % 2, m, P * t:P * (t + 1)], w2t[:, m],
                                   start=(m == 0), stop=(m == 5))
                    o.then_inc(s["m2_done"], 1)

            for c in range(NCH):
                if c + 1 < NCH:
                    second_transposes(c + 1)
                hidden(c)
                if c:
                    second_layer(c - 1)
            second_layer(NCH - 1)


def _constants():
    import numpy as np
    k = np.zeros((ROWS, 512), np.float32)
    pos = [(r, c, -1) for r in range(WS) for c in range(WS)]
    of_image = [(r, c, 0) for r in range(WS) for c in range(W - WS)]
    of_image += [(r, c % WS, 1 if c < WS else 2) for r in range(H - WS) for c in range(W)]
    cols = list(pos)
    for par in range(2):
        cols += [(r, c, w + 3 * par) for r, c, w in of_image]
    cols += [(r, c, -2) for r, c, _ in pos]
    for n, (r, c, cls) in enumerate(cols):
        for base, at in ((R_BIAS, r), (R_BIAS + WS, c), (R_BIAS + 2 * WS, r), (R_BIAS + 3 * WS, c)):
            k[base + at, n] = 1.0
        for j in range(6):
            if cls >= 0:
                allowed = j == cls
            elif cls == -2:
                real = ((c < 2), (r < 2), (r < 2 and c < 2))[j % 3]
                allowed = not real
            else:
                allowed = True
            k[R_MASK + j, n] = 0.0 if allowed else MASKED
        k[R_MAX:R_MAX + 2, n] = 1.0
    q = np.zeros((ROWS, T), np.float32)
    for p_ in range(NP):
        for n, (_, _, cls) in enumerate(cols[WIN:WIN + PAIR]):
            q[R_MASK + cls, MAIN + PAIR * p_ + n] = 1.0
    return k[R_CONST:], q[Q_CONST:]


def kernel(**inputs):
    import numpy as np
    import concourse.bacc as _bacc
    from concourse import mybir as _mybir
    from concourse.bass_utils import run_bass_kernel_spmd as _run

    i = {n.replace("L0_conv_", ""): np.ascontiguousarray(a) for n, a in inputs.items()}
    kconst, qconst = _constants()
    vectors = np.zeros((P, 32), np.float32)
    for n, name in ((0, "ln1_g"), (1, "ln1_b"), (4, "ln2_g"), (5, "ln2_b")):
        vectors[:, n] = i[name][:P]
        vectors[:C - P, n + 2] = i[name][P:]
    vectors[:, 8] = i["qkv_b"][0:P]
    vectors[:, 9] = i["qkv_b"][C:C + P]
    vectors[:64, 10] = i["qkv_b"][P:C]
    vectors[64:, 10] = i["qkv_b"][C + P:2 * C]
    vectors[:, 11:17] = i["mlp_b1"].reshape(6, P).T
    vectors[:, 17] = 1.0
    vectors[:, 18] = KD ** -0.5
    vectors[:64, 19] = 1.0
    vectors[64:, 19] = KD ** -0.5
    for h in range(A8):
        vectors[KD * h:KD * (h + 1), 24 + h] = 1.0
    rows = np.zeros((3 + HEADS, C), np.float32)
    rows[0] = i["qkv_b"][2 * C:]
    rows[1] = i["proj_b"]
    rows[2] = i["mlp_b2"]
    for h in range(HEADS):
        rows[3 + h, KD * h:KD * (h + 1)] = 1.0
    rel = np.ascontiguousarray(np.stack([i["rel_h"][::-1].T, i["rel_w"][::-1].T], axis=1))
    arrays = {"x": i["x"], "qkv_w": i["qkv_w"], "proj_w": i["proj_w"], "mlp_w1": i["mlp_w1"], "mlp_w2": i["mlp_w2"],
              "vectors": vectors, "rows": rows, "rel": rel, "kconst": kconst, "qconst": qconst,
              "ident_in": np.eye(P, dtype=np.float32)}
    nc = _bacc.Bacc("TRN2", target_bir_lowering=False, num_devices=1)
    args = {n: nc.dram_tensor(f"in_{n}", a.shape, _mybir.dt.from_np(a.dtype), kind="ExternalInput").ap()
            for n, a in arrays.items()}
    args["out"] = nc.dram_tensor("out_0", (B, H, W, C), _mybir.dt.float32, kind="ExternalOutput").ap()
    window_attention_block(nc, **args)
    r = _run(nc, [{f"in_{n}": a for n, a in arrays.items()}], core_ids=[0])
    return r.results[0]["out_0"]
```

```python
from contextlib import ExitStack

import concourse.bass as bass
from concourse import mybir

F32 = mybir.dt.float32
F32R = mybir.dt.float32r
ACT = mybir.ActivationFunctionType
ALU = mybir.AluOpType
AX = mybir.AxisListType

B, H, W, C = 8, 16, 16, 192
HEADS = 12
KD = C // HEADS
WS = 14
MLP = 768
EPS = 1e-6
NIMG = H * W
T = B * NIMG
P = 128
NT = T // P
CHUNK = 512
NCH = T // CHUNK

WIN = WS * WS
HALF = WIN // 2
SIDE = WS * (W - WS)
REST = NIMG - WIN
MAIN = B * WIN
PAIR = 2 * REST
NP = B // 2
PADS = T
KCOLS = T + WIN

R_BIAS = 3 * KD
R_MASK = R_BIAS + 4 * WS
R_MAX = R_MASK + 6
ROWS = R_MAX + 2
MASKED = -1.0e30

A8 = 8
VD = KD + 1
QUAD = 2 * WIN + PAIR
RING = 3
LEAD = 3


def natural(ap, img0, n):
    return ap[:, img0 * NIMG:(img0 + n) * NIMG].rearrange("p (i h w) -> p i h w", i=n, h=H)


def images_of(group):
    first = 4 * (group % 2) + group // 2
    return first, first + 2


def rest(ap):
    return ap[:, MAIN:T].rearrange("p (i t) -> p i t", i=B)


def window_attention_block(nc, x, qkv_w, proj_w, mlp_w1, mlp_w2, vectors, rows, rel, kconst, qconst, selector, ident_in, out):
    x_tiles = x.rearrange("b h w c -> (b h w) c").rearrange("(t p) c -> p t c", p=P)
    out_tiles = out.rearrange("b h w c -> (b h w) c").rearrange("(t p) c -> p t c", p=P)

    with ExitStack() as ctx:
        base = -(-nc.sbuf_base // 32) * 32

        def room(at, *tensors):
            placed = []
            for name, shape, *dt in tensors:
                placed.append(nc.alloc_sbuf_tensor_at(name, shape, dt[0] if dt else F32, offset=at))
                n = 4
                for k in shape[1:]:
                    n *= k
                at += -(-n // 32) * 32
            assert at <= nc.sbuf_usable_end, (at, nc.sbuf_usable_end)
            return at, placed

        def sem(name):
            return ctx.enter_context(nc.semaphore(name))

        ps = ctx.enter_context(nc.psum_tensor("ps", [P, 8, 512], F32))

        end, (ident, vec, vbias, bs, stats, mv, var, std, rstd, nmr, nmax, parts, parts_rest, shift, shift_rest, den,
              v_main, v_rest, v_pad, kst, qop0, qop1, kop0, kop1) = room(
            base, ("ident", [P, P]), ("vec", [P, 32]), ("vbias", [P, C]), ("bs", [P, 3]), ("stats", [P, NT, 6]),
            ("mv", [P, NT, 2]), ("var", [P, NT]), ("std", [P, NT]), ("rstd", [P, NT]), ("nmr", [P, NT]),
            ("nmax", [PAIR, 2, 2 * B + NP]), ("parts", [HALF, 2, 4 * B]), ("parts_rest", [PAIR, 2, 2 * NP]),
            ("shift", [4 * B, 2, HALF]), ("shift_rest", [2 * NP, 2, PAIR]), ("den", [P, HEADS // 4, 4 * QUAD // 32]),
            ("v_main", [HALF, 2 * B, HEADS, VD]), ("v_rest", [PAIR, NP, HEADS, VD]),
            ("v_pad", [HALF, HEADS, VD]), ("kst", [P, 512]), ("qop0", [ROWS, T], F32R), ("qop1", [ROWS, T], F32R),
            ("kop0", [ROWS, KCOLS], F32R), ("kop1", [ROWS, KCOLS], F32R))
        split, (hl0, hl1, hl2, bias8, bias4) = room(
            end, ("hl0", [P, 2, T]), ("hl1", [P, 2, KCOLS]), ("hl2", [P, 2, KCOLS]), ("bias8", [P, 2, 2, T]),
            ("bias4", [P, 2, T]))
        hl = (hl0, hl1, hl2)
        hi, lo = [a[:, 0] for a in hl], [a[:, 1] for a in hl]
        bias = (bias8[:, 0], bias8[:, 1], bias4)
        late, (xres, xn2, h2h, h2l, h2s, b1, gl, w10, w10h, w10l, w11, w11s, w11l, w2t, wp0, wp1, on0, rb, sel_in, sel) = room(
            end, ("xres", [P, NT, C]), ("xn2", [P, NT, C]), ("h2h", [P, 2, CHUNK], F32R), ("h2l", [P, 2, CHUNK], F32R),
            ("h2s", [P, 2, CHUNK], F32R), ("b1", [P, 6]), ("gl", [P, 2, 6, CHUNK]), ("w10", [P, MLP]), ("w10h", [P, MLP], F32R), ("w10l", [P, MLP], F32R),
            ("w11", [P, MLP]), ("w11s", [P, MLP], F32R), ("w11l", [C - P, MLP], F32R), ("w2t", [P, 6, C]),
            ("wp0", [P, C]), ("wp1", [C - P, C]), ("on0", [P, T]), ("rb", [P, 2, C]), ("sel_in", [2 * A8, 2, P]), ("sel", [2 * A8, 2, P], F32R))
        assert late <= split
        gl_at = end + 2 * 4 * NT * C + 3 * 8 * CHUNK + 32
        _, (xt, ht0, ht1, xf0, xf2, xf1, wq0, wq1, relc) = room(
            split, ("xt", [P, 2, 4, C]), ("ht0", [P, T]), ("ht1", [C - P, T]), ("xf0", [P, T]), ("xf2", [P, T]),
            ("xf1", [P, T]), ("wq0", [P, 3 * C]), ("wq1", [C - P, 3 * C]), ("relc", [P, 2, 2 * WS - 1]))
        den_parts = kst.rearrange("p (g l c) -> p g l c", g=4, l=2)
        _, (reld8, reld4) = room(split, ("reld8", [P, 2, 2 * WS - 1, A8]), ("reld4", [P, 2, 2 * WS - 1, HEADS - A8]))
        htw = (bias8[:, 0, 0], bias8[:, 1, 0])
        _, (qop2, kop2, pm, ppad, prest, osb, ot0, ot1) = room(
            split, ("qop2", [ROWS, T], F32R), ("kop2", [ROWS, KCOLS], F32R), ("pm", [HALF, 2, 2, 2 * WIN]),
            ("ppad", [HALF, 2, B * REST]), ("prest", [PAIR, B * REST]), ("osb", [P, 2, QUAD]),
            ("ot0", [P, T]), ("ot1", [C - P, T]))
        _, (on1,) = room(split, ("on1", [C - P, T]))
        rd = nc.alloc_sbuf_tensor_at("rd", [2 * A8, 2, T], F32R, offset=gl_at)
        qop, kop = (qop0, qop1, qop2), (kop0, kop1, kop2)
        xf = (xf0, xf1, xf2)

        s = {n: sem(n) for n in (
            "w_in", "rel_in", "rel_zero", "x0_in", "x1_in", "x2_in", "x3_in", "kst_in", "qst_in", "ops_const", "bs_ready", "v_ones",
            "var_ready", "std_ready", "rstd_ready", "xn_ready", "tp_done", "ht0_ready", "ht1_ready",
            "proj_done", "xf_ready", "hi_ready", "lo_ready", "bias_done", "bhi_ready", "blo_ready",
            "v_done", "v_ready", "op_in", "op_in1", "op_in2", "s_done", "max_ready", "mt_done", "shift_ready", "shift_in", "shift_in1",
            "st_done", "exp_done", "pv_done", "osb_ready", "o_in", "o_in1", "psum_zero",
            "late_in", "rden_ready", "bc_done", "on_ready", "pr_done", "pr8_done", "x2_ready", "st2_var", "st2_std", "st2_rstd", "xn2_ready",
            "tp2_done", "h2h_ready", "h2l_ready", "w1_split", "m1_done", "gl_ready", "m2_done", "y_ready", "y_out", "chain_dve", "chain_pool", "xpb_ready", "parts_ready", "rest_shift_in", "rest_shift_in1", "last_out_in", "sel_ready", "b1_done", "b1_ready", "w1_scaled", "w1_high", "last_den_in", "hidden_in", "res_ready", "rd0_in", "rd1_in", "xb2_ready", "pads_ready", "c0_in", "c1_in", "c2_in", "reld_ready", "htw_ready",
        )}
        op_in = [s["op_in"], s["op_in1"], s["op_in2"]]
        rest_shift_in = [s["rest_shift_in"], s["rest_shift_in1"]]
        shift_in = [s["shift_in"], s["shift_in1"]]
        o_in = [s["o_in"], s["o_in1"]]
        const_in = [s["c0_in"], s["c1_in"], s["c2_in"]]
        x_in = [s["x0_in"], s["x1_in"], s["x2_in"], s["x3_in"]]

        G1A, B1A, G1B, B1B, G2A, B2A, G2B, B2B = range(8)
        BQKV = 8
        BM1 = 11
        SCL = 17

        def place(h):
            if h < A8:
                return (0, KD * h), (1, KD * h)
            return (2, KD * (h - A8)), (2, 64 + KD * (h - A8))

        def bias_views(v):
            kind, b = v // 4, v % 4
            r0, r1 = (0, 112) if kind < 2 else (0, 56) if kind == 2 else (64, 120)
            bank = ps[r0:r1, 4 + v % 4, :].rearrange("p (j i t) -> p j i t", j=4, i=B)
            n = min(4, WS - 4 * b)

            def places(part):
                main = bias[min(kind, 2)][r0:r1, part]
                r = rest(main)
                main = main[:, 0:MAIN].rearrange("p (i h w) -> p i h w", i=B, h=WS)
                side = r[:, :, 0:SIDE].rearrange("p i (h w) -> p i h w", h=WS)
                low = r[:, :, SIDE:REST].rearrange("p i (h w) -> p i h w", w=W)
                if kind % 2 == 0:
                    main, side, low = (a.rearrange("p i h w -> p h i w") for a in (main, side, low))
                    return main[:, 4 * b:4 * b + n], side[:, 4 * b:4 * b + n], low
                main, side, low = (a.rearrange("p i h w -> p w i h") for a in (main, side, low))
                return main[:, 4 * b:4 * b + n], low[:, 4 * b:4 * b + 4], side
            if kind % 2 == 0:
                src = (bank[:, 0:n, :, 0:WS], bank[:, 0:n, :, WS:W], bank[:, 2:4])
            else:
                src = (bank[:, 0:n, :, 0:WS], bank[:, :, :, WS:H], bank[:, 2:4, :, 0:WS])
            return list(zip(src, places(0), places(1)))[:3 if b == 3 else 2]

        def score_bank(n):
            return (n + (n > 1) + (n > 9)) % 2

        REST_MAX_BANK, MAIN_MAX_BANK = 0, 1

        def spread_bank(j):
            return (1 + j) % 2

        def output_rows(h):
            dst, r0 = (ot0, KD * h) if h < A8 else (ot1, KD * (h - A8))
            return [(den[32 * (h % 4):32 * (h % 4) + 32, h // 4], osb[KD:P:32, h % 2])] + [
                (dst[r0:r0 + KD, QUAD * j:QUAD * (j + 1)], osb[32 * j:32 * j + KD, h % 2]) for j in range(4)]

        def operands_loaded(h):
            return 16 * sum(5 if n < A8 else 8 for n in range(h % RING, h + 1, RING))

        N_LATE, N_HIDDEN = 6 * 16, 5 * 16

        block = ctx.enter_context(nc.Block())

        @block.sync
        def _(sp):
            def load_x(c):
                sp.dma_start(xt[:, c % 2], x_tiles[:, 4 * c:4 * c + 4, :]).then_inc(x_in[c], 16)

            load_x(0)
            sp.dma_start(ident[:], ident_in).then_inc(s["w_in"], 16)
            sp.dma_start(vec[:], vectors).then_inc(s["w_in"], 16)
            load_x(1)
            for wt, r0, r1 in ((wq0, 0, P), (wq1, P, C)):
                for d0, s0, n in ((0, 0, P), (P, C, P), (2 * P, P, C - P), (2 * P + C - P, C + P, 2 * C - P)):
                    sp.dma_start(wt[:, d0:d0 + n], qkv_w[r0:r1, s0:s0 + n]).then_inc(s["w_in"], 16)
            sp.dma_start(vbias[:], rows[0:1, :].to_broadcast([P, C])).then_inc(s["w_in"], 16)
            sp.dma_start(kst[R_BIAS:ROWS, :], kconst).then_inc(s["kst_in"], 16)
            sp.dma_start(kst[0:ROWS - R_MASK, :], qconst).then_inc(s["kst_in"], 16)
            for j in range(A8):
                sp.dma_start(relc[KD * j:KD * (j + 1)], rel).then_inc(s["rel_in"], 16)
            def lay_constants(slot):
                k, q = kop[slot].bitcast(F32), qop[slot].bitcast(F32)
                for dst, n, c0, w in ((0, B, 0, WIN), (MAIN, NP, WIN, PAIR), (PADS, 1, WIN + PAIR, WIN)):
                    sp.dma_start(k[R_BIAS:ROWS, dst:dst + n * w].rearrange("p (i t) -> p i t", i=n),
                                 kst[R_BIAS:ROWS, c0:c0 + w].unsqueeze(1).to_broadcast([ROWS - R_BIAS, n, w])
                                 ).then_inc(const_in[slot], 16)
                for dst, c0, w in ((0, 0, 2 * WIN), (MAIN, 2 * WIN, PAIR)):
                    sp.dma_start(q[R_MASK:ROWS, dst:dst + NP * w].rearrange("p (i t) -> p i t", i=NP),
                                 kst[0:ROWS - R_MASK, c0:c0 + w].unsqueeze(1).to_broadcast([ROWS - R_MASK, NP, w])
                                 ).then_inc(const_in[slot], 16)

            def load_operands(h):
                (tq, rq), (tk, rk) = place(h)
                q, k, sl = qop[h % RING].bitcast(F32), kop[h % RING].bitcast(F32), op_in[h % RING]
                if h >= RING:
                    sp.wait_ge(s["st_done"], 6 * (h - RING + 1))
                if h == 0:
                    sp.wait_ge(s["lo_ready"], 18)
                    sp.wait_ge(s["hi_ready"], 18)
                    sp.wait_ge(s["pads_ready"], 4)
                src = hl[tq][rq:rq + KD, :, 0:T]
                sp.dma_start(q[0:2 * KD], src).then_inc(sl, 16)
                sp.dma_start(q[2 * KD:R_BIAS], src[:, 0]).then_inc(sl, 16)
                src = hl[tk][rk:rk + KD]
                sp.dma_start(k[0:2 * KD], src[:, 0:1].to_broadcast([KD, 2, KCOLS])).then_inc(sl, 16)
                sp.dma_start(k[2 * KD:R_BIAS], src[:, 1]).then_inc(sl, 16)
                if h == 0:
                    sp.wait_ge(s["bhi_ready"], 8)
                    sp.wait_ge(s["blo_ready"], 8)
                if h == A8:
                    sp.wait_ge(s["bhi_ready"], 16)
                    sp.wait_ge(s["blo_ready"], 16)
                if h < A8:
                    sp.dma_start(q[R_BIAS:R_MASK], bias8[h:h + A8 * (WS - 1) + 1:A8]).then_inc(sl, 16)
                else:
                    n = HEADS - A8
                    for a_ in range(2):
                        r0 = 64 * a_ + h - A8
                        for l in range(2):
                            sp.dma_start(q[R_BIAS + 2 * a_ + l:R_MASK:4], bias4[r0:r0 + n * (WS - 1) + 1:n, l]).then_inc(sl, 16)

            sp.wait_ge(s["kst_in"], 32)
            lay_constants(0)
            for c in range(2, NCH):
                sp.wait_ge(s["tp_done"], 2 * (c - 1))
                load_x(c)
            lay_constants(1)
            load_operands(0)
            load_operands(1)
            sp.wait_ge(s["bhi_ready"], 16)
            sp.wait_ge(s["blo_ready"], 16)
            lay_constants(2)
            def load_main_shifts(h):
                sp.wait_ge(s["shift_ready"], 2 * h + 1)
                sp.dma_start(qop[h % RING].bitcast(F32)[R_MAX:ROWS, 0:MAIN], shift[:, h % 2]).then_inc(shift_in[h % 2], 16)

            def load_rest_shifts(h):
                sp.wait_ge(s["shift_ready"], 2 * h + 2)
                sp.dma_start(qop[h % RING].bitcast(F32)[R_MAX:ROWS, MAIN:T], shift_rest[:, h % 2]).then_inc(rest_shift_in[h % 2], 16)

            load_main_shifts(0)
            for h in range(HEADS):
                if h + 2 < HEADS:
                    load_operands(h + 2)
                load_rest_shifts(h)
                if h + 1 < HEADS:
                    load_main_shifts(h + 1)
                if h == HEADS - 3:
                    for n in range(HEADS - RING, HEADS):
                        sp.wait_ge(op_in[n % RING], operands_loaded(n))
                    for dst, src in ((sel_in[:], selector), (rb[:, 0], rows[1:2, :].to_broadcast([P, C])),
                                     (rb[:, 1], rows[2:3, :].to_broadcast([P, C])), (wp0[:], proj_w[0:P]),
                                     (xres[:, 0:NT // 2], x_tiles[:, 0:NT // 2]), (xres[:, NT // 2:NT], x_tiles[:, NT // 2:NT])):
                        sp.dma_start(dst, src).then_inc(s["late_in"], 16)
                    sp.wait_ge(s["rden_ready"], 2)
                    for k in range(2):
                        for l in range(2):
                            sp.dma_start(rd[A8 * l + 4 * k:A8 * l + 4 * (k + 1), 0].bitcast(F32),
                                         den_parts[:, k, l]).then_inc(s["rd0_in"], 16)
                if h == HEADS - 2:
                    for dst, src in ((wp1[:], proj_w[P:C]), (w10[:], mlp_w1[0:P]), (w11[0:C - P], mlp_w1[P:C]),
                                     (w11[C - P:P], mlp_w1[P:C]), (w2t[:], mlp_w2.rearrange("(m p) c -> p m c", p=P))):
                        sp.dma_start(dst, src).then_inc(s["hidden_in"], 16)
            sp.wait_ge(s["osb_ready"], 2 * HEADS)
            for n, (dst, src) in enumerate(output_rows(HEADS - 1)):
                sp.dma_start(dst, src).then_inc(s["last_out_in"] if n else s["last_den_in"], 16)
            sp.wait_ge(s["rden_ready"], 3)
            for l in range(2):
                sp.dma_start(rd[4 * l:4 * (l + 1), 1].bitcast(F32), den_parts[:, 2, l]).then_inc(s["rd1_in"], 16)
            for t in range(0, NT, 2):
                sp.wait_ge(s["y_ready"], t // 2 + 1)
                sp.dma_start(out_tiles[:, t:t + 2], xn2[:, t:t + 2]).then_inc(s["y_out"], 16)
            sp.wait_ge(s["y_out"], 16 * (NT // 2))

        @block.gpsimd
        def _(pool):
            g = nc.gpsimd
            n_chain = [0]

            def after(ins):
                n_chain[0] += 1
                ins.then_inc(s["chain_pool"], 1)
                pool.wait_ge(s["chain_pool"], n_chain[0])


            def normalise(c):
                pool.wait_ge(x_in[c], 16)
                pool.wait_ge(s["rstd_ready"], c + 1)
                for k in range(4):
                    t = 4 * c + k
                    g.tensor_scalar(xt[:, c % 2, k], xt[:, c % 2, k], rstd[:, t:t + 1], nmr[:, t:t + 1],
                                    ALU.mult, ALU.add).then_inc(s["xn_ready"], 1)

            def split_lo(m, c):
                pool.wait_ge(s["hi_ready"], 3 * c + m + 1)
                n = slice(2 * c * WIN, 2 * (c + 1) * WIN)
                g.tensor_tensor(lo[m][:, n].rearrange("p (i h w) -> p i h w", i=2, h=WS).bitcast(F32R),
                                natural(xf[m], 2 * c, 2)[:, :, 0:WS, 0:WS],
                                hi[m][:, n].rearrange("p (i h w) -> p i h w", i=2, h=WS),
                                ALU.subtract).then_inc(s["lo_ready"], 1)

            normalise(0)
            normalise(1)
            normalise(2)
            for c in range(NCH):
                for m in range(3):
                    split_lo(m, c)
                if c == 0:
                    normalise(3)
            pool.wait_ge(s["rel_in"], 16 * A8)
            pool.wait_ge(s["tp_done"], 2 * NCH)
            for d, nh in ((reld8, A8), (reld4, HEADS - A8)):
                g.tensor_tensor(d[:].rearrange("p a r j -> p (a r) j"),
                                relc[:].rearrange("p a r -> p (a r)").unsqueeze(2).to_broadcast([P, 2 * (2 * WS - 1), nh]),
                                vec[:, 24:24 + nh].unsqueeze(1).to_broadcast([P, 2 * (2 * WS - 1), nh]),
                                ALU.mult).then_inc(s["reld_ready"], 1)
            pool.wait_ge(s["bs_ready"], 1)

            def pads(m, n):
                b_ = bs[:, m:m + 1].to_broadcast([P, WIN])
                g.tensor_copy(hi[m][:, PADS:KCOLS].bitcast(F32R), b_).then_inc(s["pads_ready"], 1)
                pool.wait_ge(s["pads_ready"], 2 * n + 1)
                g.tensor_tensor(lo[m][:, PADS:KCOLS].bitcast(F32R), b_, hi[m][:, PADS:KCOLS],
                                ALU.subtract).then_inc(s["pads_ready"], 1)

            pads(1, 0)
            pads(2, 1)

            def store_heads_output(h):
                pool.wait_ge(s["osb_ready"], 2 * (h + 1))
                for dst, src in output_rows(h):
                    pool.dma_start(dst, src).then_inc(o_in[h % 2], 16)

            for h in range(HEADS - 2):
                store_heads_output(h)

            pool.wait_ge(s["late_in"], N_LATE)
            for c in range(NCH):
                g.tensor_tensor(xres[:, 4 * c:4 * c + 4], xres[:, 4 * c:4 * c + 4],
                                rb[:, 0:1].to_broadcast([P, 4, C]), ALU.add).then_inc(s["xpb_ready"], 1)
            store_heads_output(HEADS - 2)

            pool.wait_ge(s["b1_done"], 1)
            g.tensor_scalar(w10[:], w10[:], vec[:, G2A:G2A + 1], None, ALU.mult).then_inc(s["w1_scaled"], 1)
            g.tensor_scalar(w11[:], w11[:], vec[:, G2B:G2B + 1], None, ALU.mult).then_inc(s["w1_scaled"], 1)
            pool.wait_ge(s["w1_high"], 2)
            g.tensor_tensor(w10l[:], w10[:], w10h[:], ALU.subtract).then_inc(s["w1_split"], 1)
            pool.wait_ge(s["w1_split"], 1)
            g.tensor_tensor(w11l[:], w11[0:C - P], w11s[0:C - P], ALU.subtract).then_inc(s["w1_split"], 1)
            pool.wait_ge(s["w1_split"], 2)
            for t in range(NT):
                if t % (NT // 2) == 0:
                    pool.wait_ge(s["st2_rstd"], t // (NT // 2) + 1)
                g.tensor_scalar(xn2[:, t], xres[:, t], rstd[:, t:t + 1], nmr[:, t:t + 1],
                                ALU.mult, ALU.add).then_inc(s["xn2_ready"], 1)
                if t % 4 == 3:
                    c = t // 4
                    pool.wait_ge(s["xn2_ready"], t + 1)
                    g.tensor_tensor(xres[:, 4 * c:4 * c + 4], xres[:, 4 * c:4 * c + 4],
                                    rb[:, 1:2].to_broadcast([P, 4, C]), ALU.add).then_inc(s["xb2_ready"], 1)

        @block.scalar
        def _(act):
            a = nc.scalar

            def std_of(c):
                act.wait_ge(s["var_ready"], c + 1)
                a.activation(std[:, 4 * c:4 * c + 4], var[:, 4 * c:4 * c + 4], ACT.Sqrt).then_inc(s["std_ready"], 1)

            def channels0(c):
                act.wait_ge(s["tp_done"], 2 * c + 1)
                a.activation(ht0[:, c * CHUNK:(c + 1) * CHUNK], ps[:, c % 2, :], ACT.Identity,
                             scale=vec[:, G1A:G1A + 1], bias=vec[:, B1A:B1A + 1]).then_inc(s["ht0_ready"], 1)

            def unit(m, c):
                u = 3 * c + m
                act.wait_ge(s["proj_done"], u + 1)
                a.activation(xf[m][:, c * CHUNK:(c + 1) * CHUNK], ps[:, 4 + u % 4, :], ACT.Identity,
                             scale=vec[:, SCL + m:SCL + m + 1], bias=bs[:, m:m + 1]).then_inc(s["xf_ready"], 1)

            act.wait_ge(s["w_in"], 11 * 16)
            std_of(0)
            std_of(1)
            act.wait_ge(s["bs_ready"], 1)
            for c in range(NCH):
                channels0(c)
                if c + 2 < NCH:
                    std_of(c + 2)
                for m in range(3):
                    unit(m, c)

            act.wait_ge(s["v_done"], 10)
            for v in range(16):
                act.wait_ge(s["bias_done"], v + 1)
                for src, high, _ in bias_views(v):
                    o = a.copy(high.bitcast(F32R), src)
                o.then_inc(s["bhi_ready"], 1)

            def main_shifts(h):
                act.wait_ge(s["mt_done"], 2 * h + 1)
                if h >= 2:
                    act.wait_ge(shift_in[h % 2], 16 * (h // 2))
                a.copy(shift[:, h % 2].bitcast(F32R), ps[0:4 * B, MAIN_MAX_BANK, 0:HALF]).then_inc(s["shift_ready"], 1)

            def rest_shifts(h):
                act.wait_ge(s["mt_done"], 2 * h + 2)
                if h >= 2:
                    act.wait_ge(rest_shift_in[h % 2], 16 * (h // 2))
                a.copy(shift_rest[:, h % 2].bitcast(F32R), ps[0:2 * NP, REST_MAX_BANK, 0:PAIR]).then_inc(s["shift_ready"], 1)

            def exp_group(h, gi):
                n = 6 * h + gi
                act.wait_ge(s["st_done"], n + 1)
                if h == 0 and gi == 0:
                    act.wait_ge(s["blo_ready"], 16)
                b0 = 2 + 2 * (n % 2)
                if gi < 4:
                    k = 4 * h + gi
                    if k >= 2:
                        act.wait_ge(s["pv_done"], 6 * ((k - 2) // 4) + (k - 2) % 4 + 1)
                    a.activation(pm[:, gi % 2], ps[0:HALF, b0:b0 + 2, 0:2 * WIN], ACT.Exp).then_inc(s["exp_done"], 1)
                elif gi == 4:
                    if h:
                        act.wait_ge(s["pv_done"], 6 * h)
                    a.activation(ppad[:], ps[0:HALF, b0:b0 + 2, 0:B * REST], ACT.Exp).then_inc(s["exp_done"], 1)
                else:
                    a.activation(prest[:], ps[0:PAIR, b0, 0:B * REST], ACT.Exp).then_inc(s["exp_done"], 1)

            def main_output(h):
                if h >= 2:
                    act.wait_ge(o_in[h % 2], 5 * 16 * (h // 2))
                act.wait_ge(s["pv_done"], 6 * h + 4)
                a.copy(osb[:, h % 2, 0:2 * WIN], ps[:, 6, 0:2 * WIN]).then_inc(s["osb_ready"], 1)

            def rest_output(h):
                act.wait_ge(s["pv_done"], 6 * h + 6)
                a.copy(osb[:, h % 2, 2 * WIN:QUAD], ps[:, 7, 0:PAIR]).then_inc(s["osb_ready"], 1)

            main_shifts(0)
            rest_shifts(0)
            for h in range(HEADS):
                for gi in range(6):
                    exp_group(h, gi)
                    if gi == 0 and h:
                        rest_output(h - 1)
                    if gi == (10 - LEAD) // 2 and h + 1 < HEADS:
                        main_shifts(h + 1)
                    if gi == (14 - LEAD) // 2 and h + 1 < HEADS:
                        rest_shifts(h + 1)
                main_output(h)
            rest_output(HEADS - 1)

            act.wait_ge(s["w1_scaled"], 2)
            a.copy(w10h[:], w10[:]).then_inc(s["w1_high"], 1)
            a.copy(w11s[:], w11[:]).then_inc(s["w1_high"], 1)

            def second_std(k):
                n = slice(NT // 2 * k, NT // 2 * (k + 1))
                act.wait_ge(s["st2_var"], k + 1)
                a.activation(std[:, n], var[:, n], ACT.Sqrt).then_inc(s["st2_std"], 1)

            def second_channels(c):
                if c >= 2:
                    act.wait_ge(s["m1_done"], 6 * (c - 1))
                act.wait_ge(s["tp2_done"], 2 * c + 1)
                a.copy(h2h[:, c % 2], ps[:, 6 + c % 2, :]).then_inc(s["h2h_ready"], 1)
                act.wait_ge(s["tp2_done"], 2 * c + 2)
                a.copy(h2s[0:C - P, c % 2], ps[0:C - P, c % 2, :]).then_inc(s["h2h_ready"], 1)

            second_std(0)
            second_channels(0)
            second_std(1)
            for c in range(NCH):
                for m in range(6):
                    n = 6 * c + m
                    act.wait_ge(s["m1_done"], n + 1)
                    if c >= 2 and m == 0:
                        act.wait_ge(s["m2_done"], 2 * (c - 1))
                    a.activation(gl[:, c % 2, m], ps[:, 2 + n % 2, :], ACT.Gelu,
                                 bias=b1[:, m:m + 1]).then_inc(s["gl_ready"], 1)
                    if m == 3 and c + 1 < NCH:
                        second_channels(c + 1)

        @block.vector
        def _(dve):
            v_ = nc.vector
            n_chain = [0]

            def after(ins):
                n_chain[0] += 1
                ins.then_inc(s["chain_dve"], 1)
                dve.wait_ge(s["chain_dve"], n_chain[0])

            def stats_of(src, tiles):
                for t in tiles:
                    o = v_.bn_stats(stats[:, t], src(t))
                after(o)
                for t in tiles:
                    o = v_.bn_aggr(mv[:, t], stats[:, t])
                after(o)

            def rstd_of(t0, t1):
                after(v_.reciprocal(rstd[:, t0:t1], std[:, t0:t1]))
                return v_.scalar_tensor_tensor(nmr[:, t0:t1], mv[:, t0:t1, 0], -1.0, rstd[:, t0:t1], ALU.mult, ALU.mult)

            v_.memset(nmax[:], 0.0)
            v_.memset(v_pad[:, :, KD:VD], 1.0)
            v_.memset(v_main[:, :, :, KD:VD], 1.0)
            v_.memset(v_rest[:, :, :, KD:VD], 1.0)
            dve.wait_ge(s["w_in"], 11 * 16)
            v_.tensor_tensor(bs[:], vec[:, BQKV:BQKV + 3], vec[:, SCL:SCL + 3], ALU.mult).then_inc(s["bs_ready"], 1)
            v_.tensor_copy(v_pad[:, :, 0:KD], vbias[0:HALF].rearrange("p (h d) -> p h d", h=HEADS))

            def early_stats(c):
                dve.wait_ge(x_in[c], 16)
                stats_of(lambda t: xt[:, c % 2, t - 4 * c], range(4 * c, 4 * c + 4))
                v_.tensor_scalar(var[:, 4 * c:4 * c + 4], mv[:, 4 * c:4 * c + 4, 1], EPS, None,
                                 ALU.add).then_inc(s["var_ready"], 1)

            def early_rstd(c):
                dve.wait_ge(s["std_ready"], c + 1)
                rstd_of(4 * c, 4 * c + 4).then_inc(s["rstd_ready"], 1)

            def channels1(c):
                dve.wait_ge(s["tp_done"], 2 * c + 2)
                v_.tensor_scalar(ht1[:, c * CHUNK:(c + 1) * CHUNK], ps[0:64, 2 + c % 2, :], vec[0:64, G1B:G1B + 1],
                                 vec[0:64, B1B:B1B + 1], ALU.mult, ALU.add).then_inc(s["ht1_ready"], 1)

            def split_hi(m, c):
                dve.wait_ge(s["xf_ready"], 3 * c + m + 1)
                v_.tensor_copy(hi[m][:, 2 * c * WIN:2 * (c + 1) * WIN].rearrange("p (i h w) -> p i h w", i=2, h=WS).bitcast(F32R),
                               natural(xf[m], 2 * c, 2)[:, :, 0:WS, 0:WS]).then_inc(s["hi_ready"], 1)

            def rest_views(tile_, src):
                r, n = rest(tile_), natural(src, 0, B)
                return ((r[:, :, 0:SIDE].rearrange("p i (h w) -> p i h w", h=WS), n[:, :, 0:WS, WS:W]),
                        (r[:, :, SIDE:REST].rearrange("p i (h w) -> p i h w", w=W), n[:, :, WS:H, :]))

            def window_order(c):
                dve.wait_ge(s["ht0_ready"], c + 1)
                dve.wait_ge(s["ht1_ready"], c + 1)
                for kc, (ht, r) in enumerate(((ht0, P), (ht1, C - P))):
                    v_.tensor_copy(htw[kc][0:r, 2 * c * WIN:2 * (c + 1) * WIN].rearrange("p (i h w) -> p i h w", i=2, h=WS),
                                   natural(ht, 2 * c, 2)[:, :, 0:WS, 0:WS]).then_inc(s["htw_ready"], 1)
                if c == NCH - 1:
                    for kc, (ht, r) in enumerate(((ht0, P), (ht1, C - P))):
                        for o, i in rest_views(htw[kc][0:r], ht):
                            v_.tensor_copy(o, i).then_inc(s["htw_ready"], 1)

            early_stats(0)
            early_stats(1)
            early_rstd(0)
            for c in range(NCH):
                if c + 1 < NCH:
                    early_rstd(c + 1)
                channels1(c)
                if c + 2 < NCH:
                    early_stats(c + 2)
                window_order(c)
                if c:
                    for m in range(3):
                        split_hi(m, c - 1)
            for m in range(3):
                split_hi(m, NCH - 1)
            for m in range(3):
                for o, i in rest_views(hi[m], xf[m]):
                    v_.tensor_copy(o.bitcast(F32R), i).then_inc(s["hi_ready"], 1)
            dve.wait_ge(s["hi_ready"], 18)
            for m in range(3):
                for (o, i), (h_, _) in zip(rest_views(lo[m], xf[m]), rest_views(hi[m], xf[m])):
                    v_.tensor_tensor(o.bitcast(F32R), i, h_, ALU.subtract).then_inc(s["lo_ready"], 1)

            for u in range(10):
                dve.wait_ge(s["v_done"], u + 1)
                n = HALF if u < 8 else PAIR
                src = ps[0:n, u % 4, 0:2 * C].rearrange("p (k h d) -> p k h d", k=2, h=HEADS)
                dst = v_main[:, 2 * u:2 * u + 2] if u < 8 else v_rest[:, 2 * (u - 8):2 * (u - 8) + 2]
                for k in range(2):
                    o = v_.tensor_tensor(dst[:, k, :, 0:KD], src[:, k],
                                         vbias[0:n].rearrange("p (h d) -> p h d", h=HEADS), ALU.add)
                o.then_inc(s["v_ready"], 1)

            for v in range(16):
                dve.wait_ge(s["bhi_ready"], v + 1)
                for src, high, low in bias_views(v):
                    o = v_.tensor_tensor(low.bitcast(F32R), src, high, ALU.subtract)
                o.then_inc(s["blo_ready"], 1)

            def maxima(h, n):
                k, bank = 12 * h + n, score_bank(n)
                dve.wait_ge(s["s_done"], k + 1)
                if n == 0 and h >= 2:
                    dve.wait_ge(s["mt_done"], 2 * (h - 1))
                if n < B:
                    v_.tensor_reduce(nmax[0:HALF, h % 2, 2 * n:2 * n + 2],
                                     ps[0:HALF, bank, 0:2 * WIN].rearrange("p (t k) -> p t k", t=2),
                                     AX.X, ALU.max, negate=True).then_inc(s["max_ready"], 1)
                else:
                    p_ = 2 * B + n - B
                    v_.tensor_reduce(nmax[:, h % 2, p_:p_ + 1], ps[0:PAIR, bank, 0:PAIR + WIN],
                                     AX.X, ALU.max, negate=True).then_inc(s["max_ready"], 1)

            def maxima_parts(high, low, m, n_done):
                dve.wait_ge(s["max_ready"], n_done)
                after(v_.tensor_copy(high.bitcast(F32R), m))
                v_.tensor_tensor(low.bitcast(F32R), m, high, ALU.subtract).then_inc(s["parts_ready"], 1)

            def reciprocal_parts(k):
                after(v_.reciprocal(den[:, k], den[:, k]))
                high, low = den_parts[:, k, 0], den_parts[:, k, 1]
                after(v_.tensor_copy(high.bitcast(F32R), den[:, k]))
                v_.tensor_tensor(low.bitcast(F32R), den[:, k], high, ALU.subtract).then_inc(s["rden_ready"], 1)

            for h in range(HEADS):
                for n in range(B):
                    maxima(h, n)
                p_ = parts[:, h % 2]
                maxima_parts(p_[:, 0:2 * B], p_[:, 2 * B:4 * B], nmax[0:HALF, h % 2, 0:2 * B], 12 * h + B)
                for n in range(B, 12):
                    maxima(h, n)
                p_ = parts_rest[:, h % 2]
                maxima_parts(p_[:, 0:NP], p_[:, NP:2 * NP], nmax[:, h % 2, 2 * B:2 * B + NP], 12 * (h + 1))
                if h == HEADS - 2:
                    dve.wait_ge(o_in[0], 5 * 16 * A8 // 2)
                    dve.wait_ge(o_in[1], 5 * 16 * A8 // 2)
                    for k in range(2):
                        reciprocal_parts(k)

            def tokens_of(ap, j):
                n = natural(ap, 2 * j, 2)
                return n[:, :, 0:WS, 0:WS], n[:, :, 0:WS, WS:W], n[:, :, WS:H, :]

            def in_quadrant(ap):
                r = ap[:, 2 * WIN:QUAD].rearrange("p (i t) -> p i t", i=2)
                return (ap[:, 0:2 * WIN].rearrange("p (i h w) -> p i h w", i=2, h=WS),
                        r[:, :, 0:SIDE].rearrange("p i (h w) -> p i h w", h=WS),
                        r[:, :, SIDE:REST].rearrange("p i (h w) -> p i h w", w=W))

            def normalise(k, j):
                dst, src, n = ((on0, ot0, P), (on1, ot1, C - P))[k]
                dve.wait_ge(s["bc_done"], 4 * k + j + 1)
                for d, x1, x2 in zip(tokens_of(dst[0:n], j), in_quadrant(src[0:n, QUAD * j:QUAD * (j + 1)]),
                                     in_quadrant(ps[0:n, spread_bank(j), :])):
                    o = v_.tensor_tensor(d, x1, x2, ALU.mult)
                o.then_inc(s["on_ready"], 1)

            def residual_of_eight(u):
                dve.wait_ge(s["pr8_done"], u + 1)
                dve.wait_ge(s["xpb_ready"], u // 2 + 1)
                v_.tensor_tensor(xres[:, 2 * u:2 * u + 2], ps[:, u % 2, 0:2 * C].rearrange("p (k c) -> p k c", k=2),
                                 xres[:, 2 * u:2 * u + 2], ALU.add).then_inc(s["res_ready"], 1)

            dve.wait_ge(s["late_in"], N_LATE)
            v_.tensor_copy(sel[:], sel_in[:]).then_inc(s["sel_ready"], 1)
            for j in range(4):
                normalise(0, j)
            dve.wait_ge(s["b1_done"], 1)
            v_.tensor_tensor(b1[:], ps[:, 1, 0:6], vec[:, BM1:BM1 + 6], ALU.add).then_inc(s["b1_ready"], 1)
            for u in range(NT // 2):
                residual_of_eight(u)
            dve.wait_ge(o_in[0], 5 * 16 * HEADS // 2)
            dve.wait_ge(o_in[1], 5 * 16 * (HEADS // 2 - 1))
            dve.wait_ge(s["last_den_in"], 16)
            reciprocal_parts(2)
            dve.wait_ge(s["last_out_in"], 4 * 16)

            def residual(c):
                for u in (2 * c, 2 * c + 1):
                    dve.wait_ge(s["pr_done"], u + 1)
                    dve.wait_ge(s["res_ready"], u + 1)
                    v_.tensor_tensor(xres[:, 2 * u:2 * u + 2], ps[:, 2 + u % 4, 0:2 * C].rearrange("p (k c) -> p k c", k=2),
                                     xres[:, 2 * u:2 * u + 2], ALU.add).then_inc(s["x2_ready"], 1)
                for u in (2 * c, 2 * c + 1):
                    dve.wait_ge(s["x2_ready"], u + 1)
                    for t in (2 * u, 2 * u + 1):
                        o = v_.bn_stats(stats[:, t], xres[:, t])
                after(o)
                for t in range(4 * c, 4 * c + 4):
                    o = v_.bn_aggr(mv[:, t], stats[:, t])
                if c % 2:
                    after(o)
                    n = slice(4 * c - 4, 4 * c + 4)
                    v_.tensor_scalar(var[:, n], mv[:, n, 1], EPS, None, ALU.add).then_inc(s["st2_var"], 1)

            def second_rstd(k):
                dve.wait_ge(s["st2_std"], k + 1)
                rstd_of(NT // 2 * k, NT // 2 * (k + 1)).then_inc(s["st2_rstd"], 1)

            normalise(1, 0)
            normalise(1, 1)
            residual(0)
            normalise(1, 2)
            residual(1)
            normalise(1, 3)
            second_rstd(0)
            def second_channels_lo(c):
                dve.wait_ge(s["h2h_ready"], 2 * c + 2)
                if c >= 2:
                    dve.wait_ge(s["m1_done"], 6 * (c - 1))
                v_.tensor_tensor(h2l[:, c % 2], ps[:, 6 + c % 2, :], h2h[:, c % 2], ALU.subtract).then_inc(s["h2l_ready"], 1)
                v_.tensor_tensor(h2s[C - P:P, c % 2], ps[0:C - P, c % 2, :], h2s[0:C - P, c % 2],
                                 ALU.subtract).then_inc(s["h2l_ready"], 1)

            def results(c):
                for u in (2 * c, 2 * c + 1):
                    dve.wait_ge(s["m2_done"], u + 1)
                    dve.wait_ge(s["xb2_ready"], c + 1)
                    v_.tensor_tensor(xn2[:, 2 * u:2 * u + 2], ps[:, 4 + u % 2, 0:2 * C].rearrange("p (k c) -> p k c", k=2),
                                     xres[:, 2 * u:2 * u + 2], ALU.add).then_inc(s["y_ready"], 1)

            residual(2)
            second_channels_lo(0)
            residual(3)
            second_rstd(1)
            second_channels_lo(1)
            second_channels_lo(2)
            results(0)
            second_channels_lo(3)
            for c in range(1, NCH):
                results(c)

        @block.tensor
        def _(pe):
            mm = nc.tensor.matmul

            pe.wait_ge(s["w_in"], 11 * 16)

            def transposes(c, src, ready, done, banks, evac, n):
                pe.wait_ge(ready, 4 * (c + 1))
                if c >= 2:
                    for e in evac:
                        pe.wait_ge(e, n * (c - 1))
                for k in range(4):
                    o = nc.tensor.transpose(ps[:, banks[0] + c % 2, P * k:P * (k + 1)], src(c, k)[:, 0:P], ident[:])
                o.then_inc(done, 1)
                for k in range(4):
                    o = nc.tensor.transpose(ps[0:64, banks[1] + c % 2, P * k:P * (k + 1)], src(c, k)[:, P:C], ident[:])
                o.then_inc(done, 1)

            def project(c):
                cols = slice(c * CHUNK, (c + 1) * CHUNK)
                pe.wait_ge(s["ht0_ready"], c + 1)
                pe.wait_ge(s["ht1_ready"], c + 1)
                for m in range(3):
                    u = 3 * c + m
                    if u >= 4:
                        pe.wait_ge(s["xf_ready"], u - 3)
                    for k, (wt, ht) in enumerate(((wq0, ht0), (wq1, ht1))):
                        o = mm(ps[:, 4 + u % 4, :], wt[:, P * m:P * (m + 1)], ht[:, cols], start=(k == 0), stop=(k == 1))
                    o.then_inc(s["proj_done"], 1)

            def early_src(c, k):
                return xt[:, c % 2, k]

            for c in range(NCH):
                transposes(c, early_src, s["xn_ready"], s["tp_done"], (0, 2), (s["ht0_ready"], s["ht1_ready"]), 1)
                if c:
                    project(c - 1)
            project(NCH - 1)

            for u in range(10):
                if u < 4:
                    pe.wait_ge(s["ht0_ready"], NCH)
                    pe.wait_ge(s["ht1_ready"], NCH)
                if u == 0:
                    pe.wait_ge(s["htw_ready"], 2 * NCH + 4)
                if u >= 4:
                    pe.wait_ge(s["v_ready"], u - 3)
                for k in range(2):
                    n, c0 = (HALF, HALF * (2 * u + k)) if u < 8 else (PAIR, MAIN + PAIR * (2 * (u - 8) + k))
                    for kc, (wt, r) in enumerate(((wq0, P), (wq1, C - P))):
                        o = mm(ps[0:n, u % 4, C * k:C * (k + 1)], htw[kc][0:r, c0:c0 + n], wt[:, 2 * C:3 * C],
                               start=(kc == 0), stop=(kc == 1))
                o.then_inc(s["v_done"], 1)

            pe.wait_ge(s["reld_ready"], 2)
            pe.wait_ge(s["xf_ready"], 12)
            for v in range(16):
                kind, b = v // 4, v % 4
                if v >= 4:
                    pe.wait_ge(s["blo_ready"], v - 3)
                table, nh = (reld8, A8) if kind < 2 else (reld4, HEADS - A8)
                table = table[:, kind % 2].rearrange("p r j -> p (r j)")
                part = slice(0, 112) if kind < 2 else slice(0, 56) if kind == 2 else slice(64, 120)
                src = natural(xf0 if kind < 2 else xf2, 0, B)
                for j in range(4):
                    idx = 4 * b + j
                    shift0 = WS - 1 - idx % WS
                    r = src[:, :, idx, :] if kind in (0, 2) else src[:, :, :, idx]
                    o = mm(ps[part, 4 + v % 4, P * j:P * (j + 1)], table[:, shift0 * nh:(shift0 + WS) * nh], r,
                           start=True, stop=True)
                o.then_inc(s["bias_done"], 1)

            def score_piece(h, n):
                k, bank = 12 * h + n, score_bank(n)
                q, kk = qop[h % RING], kop[h % RING]
                if n == 0:
                    pe.wait_ge(op_in[h % RING], operands_loaded(h))
                    pe.wait_ge(const_in[h % RING], 5 * 16)
                    if h == 0:
                        pe.wait_ge(s["v_ready"], 10)
                if n in (2, 10):
                    pe.wait_ge(s["max_ready"], k)
                elif n == 11:
                    pe.wait_ge(s["shift_ready"], 2 * h + 1)
                elif h and n == 3:
                    pe.wait_ge(s["shift_ready"], 2 * h)
                elif k >= 2:
                    pe.wait_ge(s["max_ready"], k - 1)
                if n < B:
                    for t in range(2):
                        o = mm(ps[0:HALF, bank, WIN * t:WIN * (t + 1)],
                               q[0:R_MASK, WIN * n + HALF * t:WIN * n + HALF * (t + 1)],
                               kk[0:R_MASK, WIN * n:WIN * (n + 1)], start=True, stop=True)
                else:
                    c0 = MAIN + PAIR * (n - B)
                    mm(ps[0:PAIR, bank, 0:PAIR], q[0:R_MAX, c0:c0 + PAIR], kk[0:R_MAX, c0:c0 + PAIR], start=True, stop=True)
                    o = mm(ps[0:PAIR, bank, PAIR:PAIR + WIN], q[0:R_MAX, c0:c0 + PAIR], kk[0:R_MAX, PADS:KCOLS],
                           start=True, stop=True)
                o.then_inc(s["s_done"], 1)

            def main_max_rows(h):
                pe.wait_ge(s["max_ready"], 12 * h + 9)
                pe.wait_ge(s["parts_ready"], 2 * h + 1)
                nc.tensor.transpose(ps[0:4 * B, MAIN_MAX_BANK, 0:HALF], parts[:, h % 2, :],
                                    ident[0:HALF, 0:HALF]).then_inc(s["mt_done"], 1)

            def rest_max_rows(h):
                pe.wait_ge(s["parts_ready"], 2 * h + 2)
                if h + 1 < HEADS:
                    pe.wait_ge(s["max_ready"], 12 * (h + 1) + 1)
                nc.tensor.transpose(ps[0:2 * NP, REST_MAX_BANK, 0:PAIR], parts_rest[:, h % 2, :],
                                    ident[0:PAIR, 0:PAIR]).then_inc(s["mt_done"], 1)

            def weights(h, gi):
                n = 6 * h + gi
                q, kk, b0 = qop[h % RING], kop[h % RING], 2 + 2 * (n % 2)
                if gi == 0:
                    pe.wait_ge(shift_in[h % 2], 16 * (h // 2 + 1))
                if gi == 4:
                    pe.wait_ge(rest_shift_in[h % 2], 16 * (h // 2 + 1))
                if n >= 2:
                    pe.wait_ge(s["exp_done"], n - 1)
                if h == 0 and gi < 2:
                    pe.wait_ge(s["blo_ready"], 16)
                if gi < 4:
                    for i in range(2):
                        img = images_of(gi)[i]
                        for t in range(2):
                            o = mm(ps[0:HALF, b0 + i, WIN * t:WIN * (t + 1)],
                                   kk[:, WIN * img + HALF * t:WIN * img + HALF * (t + 1)],
                                   q[:, WIN * img:WIN * (img + 1)], start=True, stop=True)
                elif gi == 4:
                    for t in range(2):
                        o = mm(ps[0:HALF, b0 + t, 0:B * REST], kk[:, PADS + HALF * t:PADS + HALF * (t + 1)],
                               q[:, MAIN:T], start=True, stop=True)
                else:
                    for p_ in range(NP):
                        c0 = MAIN + PAIR * p_
                        o = mm(ps[0:PAIR, b0, PAIR * p_:PAIR * (p_ + 1)], kk[:, c0:c0 + PAIR], q[:, c0:c0 + PAIR],
                               start=True, stop=True)
                o.then_inc(s["st_done"], 1)

            def sums(h, gi):
                pe.wait_ge(s["exp_done"], 6 * h + gi + 1)
                if gi == 0 and h:
                    pe.wait_ge(s["osb_ready"], 2 * h - 1)
                if gi == 4 and h:
                    pe.wait_ge(s["osb_ready"], 2 * h)
                if gi < 4:
                    for t in range(2):
                        for i in range(2):
                            img = images_of(gi)[i]
                            r0, c0 = 32 * (img // 2), WIN * (img % 2)
                            o = mm(ps[r0:r0 + VD, 6, c0:c0 + WIN], v_main[:, 2 * img + t, h, :],
                                   pm[:, gi % 2, i, WIN * t:WIN * (t + 1)], start=(t == 0), stop=(t == 1))
                elif gi == 4:
                    for t in range(2):
                        for p_ in range(NP):
                            o = mm(ps[32 * p_:32 * p_ + VD, 7, 0:PAIR], v_pad[:, h, :],
                                   ppad[:, t, PAIR * p_:PAIR * (p_ + 1)], start=(t == 0), stop=False)
                else:
                    for p_ in range(NP):
                        o = mm(ps[32 * p_:32 * p_ + VD, 7, 0:PAIR], v_rest[:, p_, h, :],
                               prest[:, PAIR * p_:PAIR * (p_ + 1)], start=False, stop=True)
                o.then_inc(s["pv_done"], 1)

            def spread(k, j):
                n, heads = ((P, A8), (C - P, HEADS - A8))[k]
                if j == 0:
                    pe.wait_ge((s["rd0_in"], s["rd1_in"])[k], (64, 32)[k])
                    pe.wait_ge(s["late_in"], N_LATE)
                    pe.wait_ge(s["sel_ready"], 1)
                    pe.wait_ge(s["shift_ready"], 2 * HEADS)
                if k == 0 and j >= 2:
                    pe.wait_ge(s["on_ready"], j - 1)
                elif k and j < 2:
                    pe.wait_ge(s["res_ready"], NT // 2)
                elif k:
                    pe.wait_ge(s["on_ready"], 4 + j - 1)
                mm(ps[0:n, spread_bank(j), :], sel[0:2 * heads, k, 0:n], rd[0:2 * heads, k, QUAD * j:QUAD * (j + 1)],
                   start=True, stop=True).then_inc(s["bc_done"], 1)

            def shift_of_hidden():
                pe.wait_ge(s["hidden_in"], N_HIDDEN)
                pe.wait_ge(s["on_ready"], 4)
                for m in range(6):
                    mm(ps[:, 1, m:m + 1], w10[:, P * m:P * (m + 1)], vec[:, B2A:B2A + 1], start=True, stop=False)
                    o = mm(ps[:, 1, m:m + 1], w11[0:C - P, P * m:P * (m + 1)], vec[0:C - P, B2B:B2B + 1], start=False, stop=True)
                o.then_inc(s["b1_done"], 1)

            def projection_of_eight(u):
                pe.wait_ge(s["on_ready"], 4)
                if u == 1:
                    pe.wait_ge(s["b1_ready"], 1)
                if u >= 2:
                    pe.wait_ge(s["res_ready"], u - 1)
                for k in range(2):
                    t = 2 * u + k
                    o = mm(ps[:, u % 2, C * k:C * (k + 1)], on0[:, P * t:P * (t + 1)], wp0[:], start=True, stop=True)
                o.then_inc(s["pr8_done"], 1)

            def scores_for_maxima(g):
                h, n = g // 12 + 1, g % 12
                if n == 10 and h < HEADS:
                    main_max_rows(h)
                if n == 2 and h <= HEADS:
                    rest_max_rows(h - 1)
                if h < HEADS:
                    score_piece(h, n)

            for n in range(12):
                score_piece(0, n)
                if n == 9:
                    main_max_rows(0)
            for g in range(LEAD):
                scores_for_maxima(g)
            for h in range(HEADS):
                for gi in range(6):
                    g = 12 * h + 2 * gi + LEAD
                    weights(h, gi)
                    scores_for_maxima(g)
                    if gi:
                        sums(h, gi - 1)
                    elif h:
                        sums(h - 1, 5)
                    scores_for_maxima(g + 1)
                    if h == HEADS - 1:
                        if gi < 4:
                            spread(0, gi)
                        elif gi == 4:
                            shift_of_hidden()
                            projection_of_eight(0)
                        else:
                            projection_of_eight(1)
            sums(HEADS - 1, 5)
            for u in range(2, NT // 2):
                projection_of_eight(u)

            def projection(c):
                for u in (2 * c, 2 * c + 1):
                    if u == 0:
                        pe.wait_ge(s["exp_done"], 6 * HEADS)
                        pe.wait_ge(s["hidden_in"], N_HIDDEN)
                    if u >= 4:
                        pe.wait_ge(s["x2_ready"], u - 3)
                    pe.wait_ge(s["on_ready"], 4 + c + 1)
                    for k in range(2):
                        t = 2 * u + k
                        o = mm(ps[:, 2 + u % 4, C * k:C * (k + 1)], on1[:, P * t:P * (t + 1)], wp1[:], start=True, stop=True)
                    o.then_inc(s["pr_done"], 1)

            spread(1, 0)
            spread(1, 1)
            projection(0)
            spread(1, 2)
            projection(1)
            spread(1, 3)
            projection(2)

            def late_src(c, k):
                return xn2[:, 4 * c + k]

            def second_transposes(c):
                if c == 0:
                    pe.wait_ge(s["osb_ready"], 2 * HEADS)
                    pe.wait_ge(s["on_ready"], 8)
                transposes(c, late_src, s["xn2_ready"], s["tp2_done"], (6, 0), (s["h2h_ready"], s["h2l_ready"]), 2)

            def hidden(c):
                pe.wait_ge(s["h2h_ready"], 2 * (c + 1))
                pe.wait_ge(s["h2l_ready"], 2 * (c + 1))
                for m in range(6):
                    n = 6 * c + m
                    if n == 0:
                        pe.wait_ge(s["w1_split"], 2)
                        pe.wait_ge(s["x2_ready"], 6)
                    if n >= 2:
                        pe.wait_ge(s["gl_ready"], n - 1)
                    terms = ((w10h, h2h[:, c % 2]), (w10l, h2h[:, c % 2]), (w10h, h2l[:, c % 2]),
                             (w11s, h2s[:, c % 2]), (w11l, h2s[0:C - P, c % 2]))
                    for i, (wt, ht) in enumerate(terms):
                        o = mm(ps[:, 2 + n % 2, :], wt[:, P * m:P * (m + 1)], ht, start=(i == 0), stop=(i == 4))
                    o.then_inc(s["m1_done"], 1)
                    if m == 2 and c + 1 < NCH:
                        second_transposes(c + 1)

            def second_layer(c):
                pe.wait_ge(s["gl_ready"], 6 * (c + 1))
                for u in (2 * c, 2 * c + 1):
                    if u == 0:
                        pe.wait_ge(s["x2_ready"], NT // 2)
                    if u >= 2:
                        pe.wait_ge(s["y_ready"], u - 1)
                    for k in range(2):
                        t = 2 * (u % 2) + k
                        for m in range(6):
                            o = mm(ps[:, 4 + u % 2, C * k:C * (k + 1)], gl[:, c % 2, m, P * t:P * (t + 1)], w2t[:, m],
                                   start=(m == 0), stop=(m == 5))
                    o.then_inc(s["m2_done"], 1)

            second_transposes(0)
            projection(3)
            for c in range(NCH):
                hidden(c)
                if c:
                    second_layer(c - 1)
            second_layer(NCH - 1)


def _constants():
    import numpy as np
    k = np.zeros((ROWS, 512), np.float32)
    pos = [(r, c, -1) for r in range(WS) for c in range(WS)]
    of_image = [(r, c, 0) for r in range(WS) for c in range(W - WS)]
    of_image += [(r, c % WS, 1 if c < WS else 2) for r in range(H - WS) for c in range(W)]
    cols = list(pos)
    for par in range(2):
        cols += [(r, c, w + 3 * par) for r, c, w in of_image]
    cols += [(r, c, -2) for r, c, _ in pos]
    for n, (r, c, cls) in enumerate(cols):
        for row in (R_BIAS + 4 * r, R_BIAS + 4 * c + 2):
            k[row:row + 2, n] = 1.0
        for j in range(6):
            if cls >= 0:
                allowed = j == cls
            elif cls == -2:
                real = ((c < 2), (r < 2), (r < 2 and c < 2))[j % 3]
                allowed = not real
            else:
                allowed = True
            k[R_MASK + j, n] = 0.0 if allowed else MASKED
        k[R_MAX:R_MAX + 2, n] = 1.0
    q = np.zeros((ROWS, 512), np.float32)
    for n, (_, _, cls) in enumerate(cols[WIN:WIN + PAIR]):
        q[R_MASK + cls, 2 * WIN + n] = 1.0
    return k[R_BIAS:], q[R_MASK:]


def kernel(**inputs):
    import numpy as np
    import concourse.bacc as _bacc
    from concourse import mybir as _mybir
    from concourse.bass_utils import run_bass_kernel_spmd as _run

    i = {n.replace("L0_conv_", ""): np.ascontiguousarray(a) for n, a in inputs.items()}
    kconst, qconst = _constants()
    vectors = np.zeros((P, 32), np.float32)
    for n, name in ((0, "ln1_g"), (1, "ln1_b"), (4, "ln2_g"), (5, "ln2_b")):
        vectors[:, n] = i[name][:P]
        vectors[:C - P, n + 2] = i[name][P:]
    vectors[P - (C - P):, 6] = i["ln2_g"][P:]
    vectors[:, 8] = i["qkv_b"][0:P]
    vectors[:, 9] = i["qkv_b"][C:C + P]
    vectors[:64, 10] = i["qkv_b"][P:C]
    vectors[64:, 10] = i["qkv_b"][C + P:2 * C]
    vectors[:, 11:17] = i["mlp_b1"].reshape(6, P).T
    vectors[:, 17] = 1.0
    vectors[:, 18] = KD ** -0.5
    vectors[:64, 19] = 1.0
    vectors[64:, 19] = KD ** -0.5
    for h in range(A8):
        vectors[KD * h:KD * (h + 1), 24 + h] = 1.0
    rows = np.zeros((3, C), np.float32)
    rows[0] = i["qkv_b"][2 * C:]
    rows[1] = i["proj_b"]
    rows[2] = i["mlp_b2"]
    selector = np.zeros((2 * A8, 2, P), np.float32)
    for h in range(A8):
        selector[h::A8, 0, KD * h:KD * (h + 1)] = 1.0
    for h in range(4):
        selector[h:8:4, 1, KD * h:KD * (h + 1)] = 1.0
    rel = np.ascontiguousarray(np.stack([i["rel_h"][::-1].T, i["rel_w"][::-1].T], axis=1))
    arrays = {"x": i["x"], "qkv_w": i["qkv_w"], "proj_w": i["proj_w"], "selector": selector, "mlp_w1": i["mlp_w1"], "mlp_w2": i["mlp_w2"],
              "vectors": vectors, "rows": rows, "rel": rel, "kconst": kconst, "qconst": qconst,
              "ident_in": np.eye(P, dtype=np.float32)}
    nc = _bacc.Bacc("TRN2", target_bir_lowering=False, num_devices=1)
    args = {n: nc.dram_tensor(f"in_{n}", a.shape, _mybir.dt.from_np(a.dtype), kind="ExternalInput").ap()
            for n, a in arrays.items()}
    args["out"] = nc.dram_tensor("out_0", (B, H, W, C), _mybir.dt.float32, kind="ExternalOutput").ap()
    window_attention_block(nc, **args)
    r = _run(nc, [{f"in_{n}": a for n, a in arrays.items()}], core_ids=[0])
    return r.results[0]["out_0"]
```

```python
from contextlib import ExitStack

import concourse.bass as bass
from concourse import mybir

F32 = mybir.dt.float32
F32R = mybir.dt.float32r
ACT = mybir.ActivationFunctionType
ALU = mybir.AluOpType
AX = mybir.AxisListType

B, H, W, C = 8, 16, 16, 192
HEADS = 12
KD = C // HEADS
WS = 14
MLP = 768
EPS = 1e-6
NIMG = H * W
T = B * NIMG
P = 128
NT = T // P
CHUNK = 512
NCH = T // CHUNK

WIN = WS * WS
HALF = WIN // 2
SIDE = WS * (W - WS)
REST = NIMG - WIN
MAIN = B * WIN
PAIR = 2 * REST
NP = B // 2
PADS = T
KCOLS = T + WIN

R_BIAS = 3 * KD
R_MASK = R_BIAS + 4 * WS
R_MAX = R_MASK + 6
ROWS = R_MAX + 2
MASKED = -1.0e30

A8 = 8
VD = KD + 1
QUAD = 2 * WIN + PAIR
RING = 3
LEAD = 3


def natural(ap, img0, n):
    return ap[:, img0 * NIMG:(img0 + n) * NIMG].rearrange("p (i h w) -> p i h w", i=n, h=H)


def images_of(group):
    first = 4 * (group % 2) + group // 2
    return first, first + 2


def rest(ap):
    return ap[:, MAIN:T].rearrange("p (i t) -> p i t", i=B)


def window_attention_block(nc, x, qkv_w, proj_w, mlp_w1, mlp_w2, vectors, rows, rel, kconst, qconst, selector,
                           ident_in, out):
    x_tiles = x.rearrange("b h w c -> (b h w) c").rearrange("(t p) c -> p t c", p=P)
    out_tiles = out.rearrange("b h w c -> (b h w) c").rearrange("(t p) c -> p t c", p=P)

    with ExitStack() as ctx:
        base = -(-nc.sbuf_base // 32) * 32

        def room(at, *tensors):
            placed = []
            for name, shape, *dt in tensors:
                placed.append(nc.alloc_sbuf_tensor_at(name, shape, dt[0] if dt else F32, offset=at))
                n = 4
                for k in shape[1:]:
                    n *= k
                at += -(-n // 32) * 32
            assert at <= nc.sbuf_usable_end, (at, nc.sbuf_usable_end)
            return at, placed

        def sem(name):
            return ctx.enter_context(nc.semaphore(name))

        ps = ctx.enter_context(nc.psum_tensor("ps", [P, 8, 512], F32))

        end, (ident, vec, vshift, bs, stats, mv, var, std, rstd, nmr, nmax, parts, parts_rest, shift, shift_rest, den,
              v_main, v_rest, v_pad, kst, qop0, qop1, kop0, kop1) = room(
            base, ("ident", [P, P]), ("vec", [P, 32]), ("vshift", [P, C]), ("bs", [P, 3]), ("stats", [P, NT, 6]),
            ("mv", [P, NT, 2]), ("var", [P, NT]), ("std", [P, NT]), ("rstd", [P, NT]), ("nmr", [P, NT]),
            ("nmax", [PAIR, 2, 2 * B + NP]), ("parts", [HALF, 2, 4 * B]), ("parts_rest", [PAIR, 2, 2 * NP]),
            ("shift", [4 * B, 2, HALF]), ("shift_rest", [2 * NP, 2, PAIR]), ("den", [P, HEADS // 4, 4 * QUAD // 32]),
            ("v_main", [HALF, 2 * B, HEADS, VD]), ("v_rest", [PAIR, NP, HEADS, VD]),
            ("v_pad", [HALF, HEADS, VD]), ("kst", [P, 512]), ("qop0", [ROWS, T], F32R), ("qop1", [ROWS, T], F32R),
            ("kop0", [ROWS, KCOLS], F32R), ("kop1", [ROWS, KCOLS], F32R))
        split, (hl0, hl1, hl2, bias8, bias4) = room(
            end, ("hl0", [P, 2, T]), ("hl1", [P, 2, KCOLS]), ("hl2", [P, 2, KCOLS]), ("bias8", [P, 2, 2, T]),
            ("bias4", [P, 2, T]))
        hl = (hl0, hl1, hl2)
        hi, lo = [a[:, 0] for a in hl], [a[:, 1] for a in hl]
        bias = (bias8[:, 0], bias8[:, 1], bias4)
        late, (xres, xn2, h2h, h2l, h2s, b1, gl, w10, w10h, w10l, w11, w11s, w11l, w2t, wp0, wp1, on0, rb,
               sel_in, sel) = room(
            end, ("xres", [P, NT, C]), ("xn2", [P, NT, C]), ("h2h", [P, 2, CHUNK], F32R), ("h2l", [P, 2, CHUNK], F32R),
            ("h2s", [P, 2, CHUNK], F32R), ("b1", [P, 6]), ("gl", [P, 2, 6, CHUNK]), ("w10", [P, MLP]),
            ("w10h", [P, MLP], F32R), ("w10l", [P, MLP], F32R),
            ("w11", [P, MLP]), ("w11s", [P, MLP], F32R), ("w11l", [C - P, MLP], F32R), ("w2t", [P, 6, C]),
            ("wp0", [P, C]), ("wp1", [C - P, C]), ("on0", [P, T]), ("rb", [P, 2, C]),
            ("sel_in", [2 * A8, 2, P]), ("sel", [2 * A8, 2, P], F32R))
        assert late <= split
        gl_at = end + 2 * 4 * NT * C + 3 * 8 * CHUNK + 32
        _, (ht0, ht1, xf0, xf2, xf1, wq0, wq1, relc, reld8, reld4, wpe0, wpe1, vb) = room(
            split, ("ht0", [P, T]), ("ht1", [C - P, T]), ("xf0", [P, T]), ("xf2", [P, T]),
            ("xf1", [P, T]), ("wq0", [P, 3 * C]), ("wq1", [C - P, 3 * C]), ("relc", [P, 2, 2 * WS - 1]),
            ("reld8", [P, 2, 2 * WS - 1, A8]), ("reld4", [P, 2, 2 * WS - 1, HEADS - A8]), ("wpe0", [P, C]),
            ("wpe1", [C - P, C]), ("vb", [P, 2, P]))
        den_parts = kst.rearrange("p (g l c) -> p g l c", g=4, l=2)
        xt = bias8[:, 0].rearrange("p l t -> p (l t)")[:, 0:NT * C].rearrange("p (t c) -> p t c", t=NT)
        htw = (bias4[:, 0], bias4[:, 1])
        _, (qop2, kop2, pm, ppad, prest, osb, ot0, ot1) = room(
            split, ("qop2", [ROWS, T], F32R), ("kop2", [ROWS, KCOLS], F32R), ("pm", [HALF, 2, 2, 2 * WIN]),
            ("ppad", [HALF, 2, B * REST]), ("prest", [PAIR, B * REST]), ("osb", [P, 2, QUAD]),
            ("ot0", [P, T]), ("ot1", [C - P, T]))
        _, (on1,) = room(split, ("on1", [C - P, T]))
        rd = nc.alloc_sbuf_tensor_at("rd", [2 * A8, 2, T], F32R, offset=gl_at)
        qop, kop = (qop0, qop1, qop2), (kop0, kop1, kop2)
        xf = (xf0, xf1, xf2)

        s = {n: sem(n) for n in (
            "w_in", "rel_in", "x0_in", "x1_in", "x2_in", "x3_in", "kst_in", "bs_ready", "var_ready",
            "std_ready", "rstd_ready", "xn_ready", "tp_done", "ht0_ready", "ht1_ready", "proj_done", "xf_ready",
            "hi_ready", "lo_ready", "bias_done", "bhi_ready", "blo_ready", "v_done", "v_ready", "op_in",
            "op_in1", "op_in2", "s_done", "max_ready", "mt_done", "shift_ready", "shift_in", "shift_in1",
            "st_done", "exp_done", "pv_done", "osb_ready", "o_in", "o_in1", "late_in", "rden_ready", "bc_done",
            "on_ready", "pr_done", "pr8_done", "x2_ready", "st2_var", "st2_std", "st2_rstd", "xn2_ready",
            "tp2_done", "h2h_ready", "h2l_ready", "w1_split", "m1_done", "gl_ready", "m2_done", "y_ready",
            "y_out", "chain_dve", "xpb_ready", "parts_ready", "rest_shift_in", "rest_shift_in1", "last_out_in",
            "vec_in", "wpe_in", "vshift_ready", "vshift_done", "rest_hi_ready", "vb_ready", "rb_ready",
            "sel_ready", "b1_done", "b1_ready", "w1_high", "last_den_in", "hidden_in", "res_ready",
            "rd0_in", "rd1_in", "xb2_ready", "pads_ready", "c0_in", "c1_in", "c2_in", "reld_ready", "htw_ready",
            "xn_early", "low_in", "low_in1", "low_in2",
        )}
        op_in = [s["op_in"], s["op_in1"], s["op_in2"]]
        rest_shift_in = [s["rest_shift_in"], s["rest_shift_in1"]]
        low_in = [s["low_in"], s["low_in1"], s["low_in2"]]
        shift_in = [s["shift_in"], s["shift_in1"]]
        o_in = [s["o_in"], s["o_in1"]]
        const_in = [s["c0_in"], s["c1_in"], s["c2_in"]]
        x_in = [s["x0_in"], s["x1_in"], s["x2_in"], s["x3_in"]]

        G1A, B1A, G1B, B1B, G2A, B2A, G2B, B2B = range(8)
        BQKV = 8
        BM1 = 11
        SCL = 17
        BV = 20

        def place(h):
            if h < A8:
                return (0, KD * h), (1, KD * h)
            return (2, KD * (h - A8)), (2, 64 + KD * (h - A8))

        def bias_views(v):
            kind, b = v // 4, v % 4
            r0, r1 = (0, 112) if kind < 2 else (0, 56) if kind == 2 else (64, 120)
            bank = ps[r0:r1, 4 + v % 4, :].rearrange("p (j i t) -> p j i t", j=4, i=B)
            n = min(4, WS - 4 * b)

            def places(part):
                main = bias[min(kind, 2)][r0:r1, part]
                r = rest(main)
                main = main[:, 0:MAIN].rearrange("p (i h w) -> p i h w", i=B, h=WS)
                side = r[:, :, 0:SIDE].rearrange("p i (h w) -> p i h w", h=WS)
                low = r[:, :, SIDE:REST].rearrange("p i (h w) -> p i h w", w=W)
                if kind % 2 == 0:
                    main, side, low = (a.rearrange("p i h w -> p h i w") for a in (main, side, low))
                    return main[:, 4 * b:4 * b + n], side[:, 4 * b:4 * b + n], low
                main, side, low = (a.rearrange("p i h w -> p w i h") for a in (main, side, low))
                return main[:, 4 * b:4 * b + n], low[:, 4 * b:4 * b + 4], side
            if kind % 2 == 0:
                src = (bank[:, 0:n, :, 0:WS], bank[:, 0:n, :, WS:W], bank[:, 2:4])
            else:
                src = (bank[:, 0:n, :, 0:WS], bank[:, :, :, WS:H], bank[:, 2:4, :, 0:WS])
            return list(zip(src, places(0), places(1)))[:3 if b == 3 else 2]

        def score_bank(n):
            return (n + (n > 1) + (n > 9)) % 2

        REST_MAX_BANK, MAIN_MAX_BANK = 0, 1
        VALUE_BANKS = (2, 3, 6, 7)

        def spread_bank(j):
            return (1 + j) % 2

        def rest_views(tile_, src):
            o, n = rest(tile_), natural(src, 0, B)
            return ((o[:, :, 0:SIDE].rearrange("p i (h w) -> p i h w", h=WS), n[:, :, 0:WS, WS:W]),
                    (o[:, :, SIDE:REST].rearrange("p i (h w) -> p i h w", w=W), n[:, :, WS:H, :]))

        def output_rows(h):
            dst, r0 = (ot0, KD * h) if h < A8 else (ot1, KD * (h - A8))
            return [(den[32 * (h % 4):32 * (h % 4) + 32, h // 4], osb[KD:P:32, h % 2])] + [
                (dst[r0:r0 + KD, QUAD * j:QUAD * (j + 1)], osb[32 * j:32 * j + KD, h % 2]) for j in range(4)]

        def low_biases_loaded(h):
            return 32 * len(range(h, A8 - 1, -RING))

        def operands_loaded(h):
            return 16 * sum(5 if n < A8 else 6 for n in range(h % RING, h + 1, RING))

        N_LATE, N_HIDDEN = 6 * 16, 5 * 16

        block = ctx.enter_context(nc.Block())

        @block.sync
        def _(sp):
            def load_x(c):
                sp.dma_start(xt[:, 4 * c:4 * c + 4], x_tiles[:, 4 * c:4 * c + 4, :]).then_inc(x_in[c], 16)

            load_x(0)
            sp.dma_start(ident[:], ident_in).then_inc(s["vec_in"], 16)
            sp.dma_start(vec[:], vectors).then_inc(s["vec_in"], 16)
            load_x(1)
            for wt, r0, r1 in ((wq0, 0, P), (wq1, P, C)):
                for d0, s0, n in ((0, 0, P), (P, C, P), (2 * P, P, C - P), (2 * P + C - P, C + P, 2 * C - P)):
                    sp.dma_start(wt[:, d0:d0 + n], qkv_w[r0:r1, s0:s0 + n]).then_inc(s["w_in"], 16)
            load_x(2)
            load_x(3)
            sp.dma_start(kst[R_BIAS:ROWS, :], kconst).then_inc(s["kst_in"], 16)
            sp.dma_start(kst[0:ROWS - R_MASK, :], qconst).then_inc(s["kst_in"], 16)
            for j in range(A8):
                sp.dma_start(relc[KD * j:KD * (j + 1)], rel).then_inc(s["rel_in"], 16)
            def lay_constants(slot):
                k, q = kop[slot].bitcast(F32), qop[slot].bitcast(F32)
                for dst, n, c0, w in ((0, B, 0, WIN), (MAIN, NP, WIN, PAIR), (PADS, 1, WIN + PAIR, WIN)):
                    sp.dma_start(k[R_BIAS:ROWS, dst:dst + n * w].rearrange("p (i t) -> p i t", i=n),
                                 kst[R_BIAS:ROWS, c0:c0 + w].unsqueeze(1).to_broadcast([ROWS - R_BIAS, n, w])
                                 ).then_inc(const_in[slot], 16)
                for dst, c0, w in ((0, 0, 2 * WIN), (MAIN, 2 * WIN, PAIR)):
                    sp.dma_start(q[R_MASK:ROWS, dst:dst + NP * w].rearrange("p (i t) -> p i t", i=NP),
                                 kst[0:ROWS - R_MASK, c0:c0 + w].unsqueeze(1).to_broadcast([ROWS - R_MASK, NP, w])
                                 ).then_inc(const_in[slot], 16)

            def load_operands(h):
                (tq, rq), (tk, rk) = place(h)
                q, k, sl = qop[h % RING].bitcast(F32), kop[h % RING].bitcast(F32), op_in[h % RING]
                if h >= RING:
                    sp.wait_ge(s["st_done"], 6 * (h - RING + 1))
                if h == 0:
                    sp.wait_ge(s["lo_ready"], 18)
                    sp.wait_ge(s["hi_ready"], 12)
                    sp.wait_ge(s["rest_hi_ready"], 6)
                    sp.wait_ge(s["pads_ready"], 4)
                src = hl[tq][rq:rq + KD, :, 0:T]
                sp.dma_start(q[0:2 * KD], src).then_inc(sl, 16)
                sp.dma_start(q[2 * KD:R_BIAS], src[:, 0]).then_inc(sl, 16)
                src = hl[tk][rk:rk + KD]
                sp.dma_start(k[0:2 * KD], src[:, 0:1].to_broadcast([KD, 2, KCOLS])).then_inc(sl, 16)
                sp.dma_start(k[2 * KD:R_BIAS], src[:, 1]).then_inc(sl, 16)
                if h == 0:
                    sp.wait_ge(s["bhi_ready"], 8)
                    sp.wait_ge(s["blo_ready"], 8)
                if h == A8:
                    sp.wait_ge(s["bhi_ready"], 16)
                    sp.wait_ge(s["blo_ready"], 16)
                if h < A8:
                    sp.dma_start(q[R_BIAS:R_MASK], bias8[h:h + A8 * (WS - 1) + 1:A8]).then_inc(sl, 16)
                else:
                    n = HEADS - A8
                    for a_ in range(2):
                        r0 = 64 * a_ + h - A8
                        sp.dma_start(q[R_BIAS + 2 * a_:R_MASK:4], bias4[r0:r0 + n * (WS - 1) + 1:n, 0]).then_inc(sl, 16)

            sp.wait_ge(s["kst_in"], 32)
            lay_constants(0)
            lay_constants(1)
            sp.dma_start(wpe0[:], proj_w[0:P]).then_inc(s["wpe_in"], 16)
            sp.dma_start(wpe1[:], proj_w[P:C]).then_inc(s["wpe_in"], 16)
            load_operands(0)
            load_operands(1)
            sp.wait_ge(s["bias_done"], 8)
            sp.wait_ge(s["htw_ready"], 2 * NCH + 4)
            lay_constants(2)
            load_operands(2)
            def load_main_shifts(h):
                sp.wait_ge(s["shift_ready"], 2 * h + 1)
                sp.dma_start(qop[h % RING].bitcast(F32)[R_MAX:ROWS, 0:MAIN], shift[:, h % 2]).then_inc(shift_in[h % 2], 16)

            def load_rest_shifts(h):
                sp.wait_ge(s["shift_ready"], 2 * h + 2)
                sp.dma_start(qop[h % RING].bitcast(F32)[R_MAX:ROWS, MAIN:T], shift_rest[:, h % 2]).then_inc(rest_shift_in[h % 2], 16)

            load_main_shifts(0)
            load_rest_shifts(0)
            sp.wait_ge(s["vshift_ready"], 1)
            for h in range(HEADS):
                if h and h + 2 < HEADS:
                    load_operands(h + 2)
                if h:
                    load_rest_shifts(h)
                if h + 1 < HEADS:
                    load_main_shifts(h + 1)
                if h == HEADS - 3:
                    for n in range(HEADS - RING, HEADS):
                        sp.wait_ge(op_in[n % RING], operands_loaded(n))
                        sp.wait_ge(low_in[n % RING], low_biases_loaded(n))
                    for dst, src in ((sel_in[:], selector), (rb[:, 0], rows[0:1, :].to_broadcast([P, C])),
                                     (rb[:, 1], rows[1:2, :].to_broadcast([P, C])), (wp0[:], proj_w[0:P]),
                                     (xres[:, 0:NT // 2], x_tiles[:, 0:NT // 2]), (xres[:, NT // 2:NT], x_tiles[:, NT // 2:NT])):
                        sp.dma_start(dst, src).then_inc(s["late_in"], 16)
                if h == HEADS - 2:
                    sp.wait_ge(s["rden_ready"], 2)
                    for k in range(2):
                        for l in range(2):
                            sp.dma_start(rd[A8 * l + 4 * k:A8 * l + 4 * (k + 1), 0].bitcast(F32),
                                         den_parts[:, k, l]).then_inc(s["rd0_in"], 16)
                    for dst, src in ((wp1[:], proj_w[P:C]), (w10[:], mlp_w1[0:P]), (w11[0:C - P], mlp_w1[P:C]),
                                     (w11[C - P:P], mlp_w1[P:C]), (w2t[:], mlp_w2.rearrange("(m p) c -> p m c", p=P))):
                        sp.dma_start(dst, src).then_inc(s["hidden_in"], 16)
            sp.wait_ge(s["osb_ready"], 2 * HEADS)
            for n, (dst, src) in enumerate(output_rows(HEADS - 1)):
                sp.dma_start(dst, src).then_inc(s["last_out_in"] if n else s["last_den_in"], 16)
            sp.wait_ge(s["rden_ready"], 3)
            for l in range(2):
                sp.dma_start(rd[4 * l:4 * (l + 1), 1].bitcast(F32), den_parts[:, 2, l]).then_inc(s["rd1_in"], 16)
            for t in range(0, NT, 2):
                sp.wait_ge(s["y_ready"], t // 2 + 1)
                sp.dma_start(out_tiles[:, t:t + 2], xn2[:, t:t + 2]).then_inc(s["y_out"], 16)
            sp.wait_ge(s["y_out"], 16 * (NT // 2))

        @block.gpsimd
        def _(pool):
            g = nc.gpsimd
            def normalise(c):
                pool.wait_ge(x_in[c], 16)
                pool.wait_ge(s["rstd_ready"], c + 1)
                for k in range(4):
                    t = 4 * c + k
                    g.tensor_scalar(xt[:, 4 * c + k], xt[:, 4 * c + k], rstd[:, t:t + 1], nmr[:, t:t + 1],
                                    ALU.mult, ALU.add).then_inc(s["xn_ready"], 1)

            def split_lo(m, c):
                pool.wait_ge(s["hi_ready"], 3 * c + m + 1)
                n = slice(2 * c * WIN, 2 * (c + 1) * WIN)
                g.tensor_tensor(lo[m][:, n].rearrange("p (i h w) -> p i h w", i=2, h=WS).bitcast(F32R),
                                natural(xf[m], 2 * c, 2)[:, :, 0:WS, 0:WS],
                                hi[m][:, n].rearrange("p (i h w) -> p i h w", i=2, h=WS),
                                ALU.subtract).then_inc(s["lo_ready"], 1)

            def relative_tables():
                pool.wait_ge(s["rel_in"], 16 * A8)
                for d, nh in ((reld8, A8), (reld4, HEADS - A8)):
                    g.tensor_tensor(d[:].rearrange("p a r j -> p (a r) j"),
                                    relc[:].rearrange("p a r -> p (a r)").unsqueeze(2).to_broadcast([P, 2 * (2 * WS - 1), nh]),
                                    vec[:, 24:24 + nh].unsqueeze(1).to_broadcast([P, 2 * (2 * WS - 1), nh]),
                                    ALU.mult).then_inc(s["reld_ready"], 1)

            normalise(2)
            normalise(3)
            relative_tables()
            for c in range(NCH):
                for m in range(3):
                    split_lo(m, c)
            pool.wait_ge(s["bs_ready"], 1)

            def pads(m, n):
                b_ = bs[:, m:m + 1].to_broadcast([P, WIN])
                g.tensor_copy(hi[m][:, PADS:KCOLS].bitcast(F32R), b_).then_inc(s["pads_ready"], 1)
                pool.wait_ge(s["pads_ready"], 2 * n + 1)
                g.tensor_tensor(lo[m][:, PADS:KCOLS].bitcast(F32R), b_, hi[m][:, PADS:KCOLS],
                                ALU.subtract).then_inc(s["pads_ready"], 1)

            pads(1, 0)
            pads(2, 1)

            def store_heads_output(h):
                pool.wait_ge(s["osb_ready"], 2 * (h + 1))
                for dst, src in output_rows(h):
                    pool.dma_start(dst, src).then_inc(o_in[h % 2], 16)

            def load_low_biases(h):
                n = HEADS - A8
                pool.wait_ge(s["st_done"], 6 * (h - RING + 1))
                pool.wait_ge(s["blo_ready"], 16)
                for a_ in range(2):
                    r0 = 64 * a_ + h - A8
                    pool.dma_start(qop[h % RING].bitcast(F32)[R_BIAS + 2 * a_ + 1:R_MASK:4],
                                   bias4[r0:r0 + n * (WS - 1) + 1:n, 1]).then_inc(low_in[h % RING], 16)

            for h in range(HEADS - 2):
                if A8 <= h + RING < HEADS:
                    load_low_biases(h + RING)
                store_heads_output(h)

            pool.wait_ge(s["late_in"], N_LATE)
            g.tensor_tensor(rb[:, 0], rb[:, 0], vshift[:], ALU.add).then_inc(s["rb_ready"], 1)
            pool.wait_ge(s["rb_ready"], 1)
            for c in range(NCH):
                g.tensor_tensor(xres[:, 4 * c:4 * c + 4], xres[:, 4 * c:4 * c + 4],
                                rb[:, 0:1].to_broadcast([P, 4, C]), ALU.add).then_inc(s["xpb_ready"], 1)
            store_heads_output(HEADS - 2)

            for t in range(NT):
                if t % 4 == 0:
                    pool.wait_ge(s["st2_rstd"], t // 4 + 1)
                g.tensor_scalar(xn2[:, t], xres[:, t], rstd[:, t:t + 1], nmr[:, t:t + 1],
                                ALU.mult, ALU.add).then_inc(s["xn2_ready"], 1)
                if t % 4 == 3:
                    c = t // 4
                    pool.wait_ge(s["xn2_ready"], t + 1)
                    g.tensor_tensor(xres[:, 4 * c:4 * c + 4], xres[:, 4 * c:4 * c + 4],
                                    rb[:, 1:2].to_broadcast([P, 4, C]), ALU.add).then_inc(s["xb2_ready"], 1)

        @block.scalar
        def _(act):
            a = nc.scalar

            def std_of(c):
                act.wait_ge(s["var_ready"], c + 1)
                a.activation(std[:, 4 * c:4 * c + 4], var[:, 4 * c:4 * c + 4], ACT.Sqrt).then_inc(s["std_ready"], 1)

            def channels0(c):
                act.wait_ge(s["tp_done"], 2 * c + 1)
                a.activation(ht0[:, c * CHUNK:(c + 1) * CHUNK], ps[:, c % 2, :], ACT.Identity,
                             scale=vec[:, G1A:G1A + 1], bias=vec[:, B1A:B1A + 1]).then_inc(s["ht0_ready"], 1)

            def unit(m, c):
                u = 3 * c + m
                act.wait_ge(s["proj_done"], u + 1)
                a.activation(xf[m][:, c * CHUNK:(c + 1) * CHUNK], ps[:, 4 + u % 4, :], ACT.Identity,
                             scale=vec[:, SCL + m:SCL + m + 1], bias=bs[:, m:m + 1]).then_inc(s["xf_ready"], 1)

            act.wait_ge(s["vec_in"], 2 * 16)
            std_of(0)
            std_of(1)
            act.wait_ge(s["bs_ready"], 1)
            channels0(0)
            std_of(2)
            std_of(3)
            for c in range(NCH):
                for m in range(3):
                    if m == 2 and c + 1 < NCH:
                        channels0(c + 1)
                    unit(m, c)
                    if c == NCH - 1:
                        act.wait_ge(s["xf_ready"], 3 * c + m + 1)
                        for o, i in rest_views(hi[m], xf[m]):
                            a.copy(o.bitcast(F32R), i).then_inc(s["rest_hi_ready"], 1)

            def bias_hi(v):
                act.wait_ge(s["bias_done"], v + 1)
                for src, high, _ in bias_views(v):
                    o = a.copy(high.bitcast(F32R), src)
                o.then_inc(s["bhi_ready"], 1)

            for v in range(8):
                bias_hi(v)
            for u in range(10):
                act.wait_ge(s["v_done"], u + 1)
                n = HALF if u < 8 else PAIR
                src = ps[0:n, VALUE_BANKS[u % 4], 0:2 * C].rearrange("p (k h d) -> p k h d", k=2, h=HEADS)
                dst = v_main[:, 2 * u:2 * u + 2] if u < 8 else v_rest[:, 2 * (u - 8):2 * (u - 8) + 2]
                for k in range(2):
                    o = a.copy(dst[:, k, :, 0:KD], src[:, k])
                o.then_inc(s["v_ready"], 1)
            act.wait_ge(s["vshift_done"], 1)
            a.copy(vshift[:], ps[:, 2, 0:C]).then_inc(s["vshift_ready"], 1)
            for v in range(8, 12):
                bias_hi(v)

            def main_shifts(h):
                act.wait_ge(s["mt_done"], 2 * h + 1)
                if h >= 2:
                    act.wait_ge(shift_in[h % 2], 16 * (h // 2))
                a.copy(shift[:, h % 2].bitcast(F32R), ps[0:4 * B, MAIN_MAX_BANK, 0:HALF]).then_inc(s["shift_ready"], 1)

            def rest_shifts(h):
                act.wait_ge(s["mt_done"], 2 * h + 2)
                if h >= 2:
                    act.wait_ge(rest_shift_in[h % 2], 16 * (h // 2))
                a.copy(shift_rest[:, h % 2].bitcast(F32R), ps[0:2 * NP, REST_MAX_BANK, 0:PAIR]).then_inc(s["shift_ready"], 1)

            def exp_group(h, gi):
                n = 6 * h + gi
                act.wait_ge(s["st_done"], n + 1)
                if h == 0 and gi == 0:
                    act.wait_ge(s["blo_ready"], 16)
                b0 = 2 + 2 * (n % 2)
                if gi < 4:
                    k = 4 * h + gi
                    if k >= 2:
                        act.wait_ge(s["pv_done"], 6 * ((k - 2) // 4) + (k - 2) % 4 + 1)
                    a.activation(pm[:, gi % 2], ps[0:HALF, b0:b0 + 2, 0:2 * WIN], ACT.Exp).then_inc(s["exp_done"], 1)
                elif gi == 4:
                    if h:
                        act.wait_ge(s["pv_done"], 6 * h)
                    a.activation(ppad[:], ps[0:HALF, b0:b0 + 2, 0:B * REST], ACT.Exp).then_inc(s["exp_done"], 1)
                else:
                    a.activation(prest[:], ps[0:PAIR, b0, 0:B * REST], ACT.Exp).then_inc(s["exp_done"], 1)

            def main_output(h):
                if h >= 2:
                    act.wait_ge(o_in[h % 2], 5 * 16 * (h // 2))
                act.wait_ge(s["pv_done"], 6 * h + 4)
                a.copy(osb[:, h % 2, 0:2 * WIN], ps[:, 6, 0:2 * WIN]).then_inc(s["osb_ready"], 1)

            def rest_output(h):
                act.wait_ge(s["pv_done"], 6 * h + 6)
                a.copy(osb[:, h % 2, 2 * WIN:QUAD], ps[:, 7, 0:PAIR]).then_inc(s["osb_ready"], 1)

            main_shifts(0)
            for v in range(12, 16):
                bias_hi(v)
            rest_shifts(0)
            def hidden_weights_high():
                act.wait_ge(s["hidden_in"], N_HIDDEN)
                a.activation(w10h[:], w10[:], ACT.Identity, scale=vec[:, G2A:G2A + 1]).then_inc(s["w1_high"], 1)
                a.activation(w11s[:], w11[:], ACT.Identity, scale=vec[:, G2B:G2B + 1]).then_inc(s["w1_high"], 1)

            for h in range(HEADS):
                for gi in range(6):
                    exp_group(h, gi)
                    if h == HEADS - 1 and gi == 3:
                        hidden_weights_high()
                    if gi == 0 and h:
                        rest_output(h - 1)
                    if gi == (10 - LEAD) // 2 and h + 1 < HEADS:
                        main_shifts(h + 1)
                    if gi == (14 - LEAD) // 2 and h + 1 < HEADS:
                        rest_shifts(h + 1)
                main_output(h)
            rest_output(HEADS - 1)

            def second_std(k):
                n = slice(4 * k, 4 * (k + 1))
                act.wait_ge(s["st2_var"], k + 1)
                a.activation(std[:, n], var[:, n], ACT.Sqrt).then_inc(s["st2_std"], 1)

            def second_channels(c):
                if c >= 2:
                    act.wait_ge(s["m1_done"], 6 * (c - 1))
                act.wait_ge(s["tp2_done"], 2 * c + 1)
                a.copy(h2h[:, c % 2], ps[:, 6 + c % 2, :]).then_inc(s["h2h_ready"], 1)
                act.wait_ge(s["tp2_done"], 2 * c + 2)
                a.copy(h2s[0:C - P, c % 2], ps[0:C - P, c % 2, :]).then_inc(s["h2h_ready"], 1)

            second_std(0)
            second_std(1)
            second_channels(0)
            second_std(2)
            second_std(3)
            for c in range(NCH):
                for m in range(6):
                    n = 6 * c + m
                    act.wait_ge(s["m1_done"], n + 1)
                    if c >= 2 and m == 0:
                        act.wait_ge(s["m2_done"], 2 * (c - 1))
                    a.activation(gl[:, c % 2, m], ps[:, 2 + n % 2, :], ACT.Gelu,
                                 bias=b1[:, m:m + 1]).then_inc(s["gl_ready"], 1)
                    if m == 2 and c + 1 < NCH:
                        second_channels(c + 1)

        @block.vector
        def _(dve):
            v_ = nc.vector
            n_chain = [0]

            def after(ins):
                n_chain[0] += 1
                ins.then_inc(s["chain_dve"], 1)
                dve.wait_ge(s["chain_dve"], n_chain[0])

            def stats_of(src, tiles):
                for t in tiles:
                    o = v_.bn_stats(stats[:, t], src(t))
                after(o)
                for t in tiles:
                    o = v_.bn_aggr(mv[:, t], stats[:, t])
                after(o)

            def rstd_of(t0, t1):
                after(v_.reciprocal(rstd[:, t0:t1], std[:, t0:t1]))
                return v_.scalar_tensor_tensor(nmr[:, t0:t1], mv[:, t0:t1, 0], -1.0, rstd[:, t0:t1], ALU.mult, ALU.mult)

            v_.memset(nmax[:], 0.0)
            v_.memset(v_pad[:, :, 0:KD], 0.0)
            v_.memset(v_pad[:, :, KD:VD], 1.0)
            v_.memset(v_main[:, :, :, KD:VD], 1.0)
            v_.memset(v_rest[:, :, :, KD:VD], 1.0)
            dve.wait_ge(s["vec_in"], 2 * 16)
            v_.tensor_tensor(bs[:], vec[:, BQKV:BQKV + 3], vec[:, SCL:SCL + 3], ALU.mult).then_inc(s["bs_ready"], 1)

            def early_stats(c):
                dve.wait_ge(x_in[c], 16)
                stats_of(lambda t: xt[:, t], range(4 * c, 4 * c + 4))
                v_.tensor_scalar(var[:, 4 * c:4 * c + 4], mv[:, 4 * c:4 * c + 4, 1], EPS, None,
                                 ALU.add).then_inc(s["var_ready"], 1)

            def early_rstd(c):
                dve.wait_ge(s["std_ready"], c + 1)
                rstd_of(4 * c, 4 * c + 4).then_inc(s["rstd_ready"], 1)

            def channels1(c):
                dve.wait_ge(s["tp_done"], 2 * c + 2)
                v_.tensor_scalar(ht1[:, c * CHUNK:(c + 1) * CHUNK], ps[0:64, 2 + c % 2, :], vec[0:64, G1B:G1B + 1],
                                 vec[0:64, B1B:B1B + 1], ALU.mult, ALU.add).then_inc(s["ht1_ready"], 1)

            def split_hi(m, c):
                dve.wait_ge(s["xf_ready"], 3 * c + m + 1)
                v_.tensor_copy(hi[m][:, 2 * c * WIN:2 * (c + 1) * WIN].rearrange("p (i h w) -> p i h w", i=2, h=WS).bitcast(F32R),
                               natural(xf[m], 2 * c, 2)[:, :, 0:WS, 0:WS]).then_inc(s["hi_ready"], 1)

            def window_order(c):
                dve.wait_ge(s["ht0_ready"], c + 1)
                dve.wait_ge(s["ht1_ready"], c + 1)
                for kc, (ht, r) in enumerate(((ht0, P), (ht1, C - P))):
                    v_.tensor_copy(htw[kc][0:r, 2 * c * WIN:2 * (c + 1) * WIN].rearrange("p (i h w) -> p i h w", i=2, h=WS),
                                   natural(ht, 2 * c, 2)[:, :, 0:WS, 0:WS]).then_inc(s["htw_ready"], 1)
                if c == NCH - 1:
                    for kc, (ht, r) in enumerate(((ht0, P), (ht1, C - P))):
                        for o, i in rest_views(htw[kc][0:r], ht):
                            v_.tensor_copy(o, i).then_inc(s["htw_ready"], 1)

            def normalise_early(c):
                dve.wait_ge(s["rstd_ready"], c + 1)
                for t in range(4 * c, 4 * c + 4):
                    v_.tensor_scalar(xt[:, t], xt[:, t], rstd[:, t:t + 1], nmr[:, t:t + 1],
                                     ALU.mult, ALU.add).then_inc(s["xn_early"], 1)

            early_stats(0)
            early_stats(1)
            for c in (0, 1):
                early_rstd(c)
                normalise_early(c)
            channels1(0)
            early_stats(2)
            early_stats(3)
            early_rstd(2)
            early_rstd(3)
            for c in range(NCH):
                if c:
                    channels1(c)
                window_order(c)
                if c:
                    for m in range(3):
                        split_hi(m, c - 1)
            for m in range(3):
                split_hi(m, NCH - 1)
            for m in range(3):
                dve.wait_ge(s["rest_hi_ready"], 2 * m + 2)
                for (o, i), (h_, _) in zip(rest_views(lo[m], xf[m]), rest_views(hi[m], xf[m])):
                    v_.tensor_tensor(o.bitcast(F32R), i, h_, ALU.subtract).then_inc(s["lo_ready"], 1)
            v_.tensor_copy(vb[:, 0], vec[:, BV:BV + 1].to_broadcast([P, P]))
            v_.tensor_copy(vb[:, 1], vec[:, BV + 1:BV + 2].to_broadcast([P, P])).then_inc(s["vb_ready"], 1)

            def bias_lo(v):
                dve.wait_ge(s["bhi_ready"], v + 1)
                if v == 8:
                    dve.wait_ge(s["v_done"], 10)
                for src, high, low in bias_views(v):
                    o = v_.tensor_tensor(low.bitcast(F32R), src, high, ALU.subtract)
                o.then_inc(s["blo_ready"], 1)

            for v in range(8):
                bias_lo(v)

            def maxima(h, n):
                k, bank = 12 * h + n, score_bank(n)
                dve.wait_ge(s["s_done"], k + 1)
                if n == 0 and h >= 2:
                    dve.wait_ge(s["mt_done"], 2 * (h - 1))
                if n < B:
                    v_.tensor_reduce(nmax[0:HALF, h % 2, 2 * n:2 * n + 2],
                                     ps[0:HALF, bank, 0:2 * WIN].rearrange("p (t k) -> p t k", t=2),
                                     AX.X, ALU.max, negate=True).then_inc(s["max_ready"], 1)
                else:
                    p_ = 2 * B + n - B
                    v_.tensor_reduce(nmax[:, h % 2, p_:p_ + 1], ps[0:PAIR, bank, 0:PAIR + WIN],
                                     AX.X, ALU.max, negate=True).then_inc(s["max_ready"], 1)

            def maxima_parts(high, low, m, n_done):
                dve.wait_ge(s["max_ready"], n_done)
                after(v_.tensor_copy(high.bitcast(F32R), m))
                v_.tensor_tensor(low.bitcast(F32R), m, high, ALU.subtract).then_inc(s["parts_ready"], 1)

            def reciprocal_parts(k):
                after(v_.reciprocal(den[:, k], den[:, k]))
                high, low = den_parts[:, k, 0], den_parts[:, k, 1]
                after(v_.tensor_copy(high.bitcast(F32R), den[:, k]))
                v_.tensor_tensor(low.bitcast(F32R), den[:, k], high, ALU.subtract).then_inc(s["rden_ready"], 1)

            for h in range(HEADS):
                for n in range(B):
                    maxima(h, n)
                    if h == 0 and n >= 6:
                        bias_lo(n + 2)
                    if h == 1 and n in (0, 1):
                        bias_lo(n + 14)
                p_ = parts[:, h % 2]
                maxima_parts(p_[:, 0:2 * B], p_[:, 2 * B:4 * B], nmax[0:HALF, h % 2, 0:2 * B], 12 * h + B)
                if h in (HEADS - 3, HEADS - 2):
                    k = h - HEADS + 3
                    for par in range(2):
                        dve.wait_ge(o_in[par], 5 * 16 * 2 * (k + 1))
                    reciprocal_parts(k)
                for n in range(B, 12):
                    maxima(h, n)
                    if h == 0:
                        bias_lo(n + 2)
                p_ = parts_rest[:, h % 2]
                maxima_parts(p_[:, 0:NP], p_[:, NP:2 * NP], nmax[:, h % 2, 2 * B:2 * B + NP], 12 * (h + 1))

            def tokens_of(ap, j):
                n = natural(ap, 2 * j, 2)
                return n[:, :, 0:WS, 0:WS], n[:, :, 0:WS, WS:W], n[:, :, WS:H, :]

            def in_quadrant(ap):
                r = ap[:, 2 * WIN:QUAD].rearrange("p (i t) -> p i t", i=2)
                return (ap[:, 0:2 * WIN].rearrange("p (i h w) -> p i h w", i=2, h=WS),
                        r[:, :, 0:SIDE].rearrange("p i (h w) -> p i h w", h=WS),
                        r[:, :, SIDE:REST].rearrange("p i (h w) -> p i h w", w=W))

            def normalise(k, j):
                dst, src, n = ((on0, ot0, P), (on1, ot1, C - P))[k]
                dve.wait_ge(s["bc_done"], 4 * k + j + 1)
                for d, x1, x2 in zip(tokens_of(dst[0:n], j), in_quadrant(src[0:n, QUAD * j:QUAD * (j + 1)]),
                                     in_quadrant(ps[0:n, spread_bank(j), :])):
                    o = v_.tensor_tensor(d, x1, x2, ALU.mult)
                o.then_inc(s["on_ready"], 1)

            def residual_of_eight(u):
                dve.wait_ge(s["pr8_done"], u + 1)
                dve.wait_ge(s["xpb_ready"], u // 2 + 1)
                v_.tensor_tensor(xres[:, 2 * u:2 * u + 2], ps[:, u % 2, 0:2 * C].rearrange("p (k c) -> p k c", k=2),
                                 xres[:, 2 * u:2 * u + 2], ALU.add).then_inc(s["res_ready"], 1)

            dve.wait_ge(s["late_in"], N_LATE)
            v_.tensor_copy(sel[:], sel_in[:]).then_inc(s["sel_ready"], 1)
            for j in range(4):
                normalise(0, j)
            dve.wait_ge(s["w1_high"], 2)
            v_.scalar_tensor_tensor(w10l[:], w10[:], vec[:, G2A:G2A + 1], w10h[:], ALU.mult,
                                    ALU.subtract).then_inc(s["w1_split"], 1)
            v_.scalar_tensor_tensor(w11l[:], w11[0:C - P], vec[0:C - P, G2B:G2B + 1], w11s[0:C - P], ALU.mult,
                                    ALU.subtract).then_inc(s["w1_split"], 1)
            for u in range(NT // 2):
                residual_of_eight(u)
                if u == 5:
                    dve.wait_ge(o_in[0], 5 * 16 * HEADS // 2)
                    dve.wait_ge(o_in[1], 5 * 16 * (HEADS // 2 - 1))
                    dve.wait_ge(s["last_den_in"], 16)
                    reciprocal_parts(2)
            dve.wait_ge(s["b1_done"], 1)
            v_.tensor_tensor(b1[:], ps[:, 2, 0:6], vec[:, BM1:BM1 + 6], ALU.add).then_inc(s["b1_ready"], 1)
            dve.wait_ge(s["last_out_in"], 4 * 16)

            def residual(c):
                for u in (2 * c, 2 * c + 1):
                    dve.wait_ge(s["pr_done"], u + 1)
                    dve.wait_ge(s["res_ready"], u + 1)
                    v_.tensor_tensor(xres[:, 2 * u:2 * u + 2], ps[:, 2 + u % 4, 0:2 * C].rearrange("p (k c) -> p k c", k=2),
                                     xres[:, 2 * u:2 * u + 2], ALU.add).then_inc(s["x2_ready"], 1)
                for u in (2 * c, 2 * c + 1):
                    dve.wait_ge(s["x2_ready"], u + 1)
                    for t in (2 * u, 2 * u + 1):
                        o = v_.bn_stats(stats[:, t], xres[:, t])
                after(o)
                for t in range(4 * c, 4 * c + 4):
                    o = v_.bn_aggr(mv[:, t], stats[:, t])
                after(o)
                n = slice(4 * c, 4 * c + 4)
                v_.tensor_scalar(var[:, n], mv[:, n, 1], EPS, None, ALU.add).then_inc(s["st2_var"], 1)

            def second_rstd(c):
                dve.wait_ge(s["st2_std"], c + 1)
                rstd_of(4 * c, 4 * (c + 1)).then_inc(s["st2_rstd"], 1)

            normalise(1, 0)
            normalise(1, 1)
            residual(0)
            normalise(1, 2)
            second_rstd(0)
            residual(1)
            normalise(1, 3)
            second_rstd(1)
            def second_channels_lo(c):
                dve.wait_ge(s["h2h_ready"], 2 * c + 2)
                if c >= 2:
                    dve.wait_ge(s["m1_done"], 6 * (c - 1))
                v_.tensor_tensor(h2l[:, c % 2], ps[:, 6 + c % 2, :], h2h[:, c % 2], ALU.subtract).then_inc(s["h2l_ready"], 1)
                v_.tensor_tensor(h2s[C - P:P, c % 2], ps[0:C - P, c % 2, :], h2s[0:C - P, c % 2],
                                 ALU.subtract).then_inc(s["h2l_ready"], 1)

            def results(c):
                for u in (2 * c, 2 * c + 1):
                    dve.wait_ge(s["m2_done"], u + 1)
                    dve.wait_ge(s["xb2_ready"], c + 1)
                    v_.tensor_tensor(xn2[:, 2 * u:2 * u + 2], ps[:, 4 + u % 2, 0:2 * C].rearrange("p (k c) -> p k c", k=2),
                                     xres[:, 2 * u:2 * u + 2], ALU.add).then_inc(s["y_ready"], 1)

            residual(2)
            second_channels_lo(0)
            second_rstd(2)
            residual(3)
            second_rstd(3)
            second_channels_lo(1)
            second_channels_lo(2)
            results(0)
            second_channels_lo(3)
            for c in range(1, NCH):
                results(c)

        @block.tensor
        def _(pe):
            mm = nc.tensor.matmul

            pe.wait_ge(s["vec_in"], 2 * 16)

            def transposes(c, src, done, banks, evac, n):
                if c >= 2:
                    for e in evac:
                        pe.wait_ge(e, n * (c - 1))
                for k in range(4):
                    o = nc.tensor.transpose(ps[:, banks[0] + c % 2, P * k:P * (k + 1)], src(c, k)[:, 0:P], ident[:])
                o.then_inc(done, 1)
                for k in range(4):
                    o = nc.tensor.transpose(ps[0:64, banks[1] + c % 2, P * k:P * (k + 1)], src(c, k)[:, P:C], ident[:])
                o.then_inc(done, 1)

            def project(c):
                cols = slice(c * CHUNK, (c + 1) * CHUNK)
                pe.wait_ge(s["w_in"], 8 * 16)
                pe.wait_ge(s["ht0_ready"], c + 1)
                pe.wait_ge(s["ht1_ready"], c + 1)
                for m in range(3):
                    u = 3 * c + m
                    if u >= 4:
                        pe.wait_ge(s["xf_ready"], u - 3)
                    for k, (wt, ht) in enumerate(((wq0, ht0), (wq1, ht1))):
                        o = mm(ps[:, 4 + u % 4, :], wt[:, P * m:P * (m + 1)], ht[:, cols], start=(k == 0), stop=(k == 1))
                    o.then_inc(s["proj_done"], 1)

            def early_src(c, k):
                return xt[:, 4 * c + k]

            for c in range(NCH):
                if c < 2:
                    pe.wait_ge(s["xn_early"], 4 * (c + 1))
                else:
                    pe.wait_ge(s["xn_ready"], 4 * (c - 1))
                transposes(c, early_src, s["tp_done"], (0, 2), (s["ht0_ready"], s["ht1_ready"]), 1)
                if c:
                    project(c - 1)
            project(NCH - 1)

            def relative_bias(v):
                kind, b = v // 4, v % 4
                if v == 0:
                    pe.wait_ge(s["reld_ready"], 2)
                if v < 4:
                    pe.wait_ge(s["xf_ready"], max(10, 9 + v))
                if v >= 4:
                    pe.wait_ge(s["blo_ready"], v - 3)
                if v in (10, 11):
                    pe.wait_ge(s["v_ready"], 10)
                table, nh = (reld8, A8) if kind < 2 else (reld4, HEADS - A8)
                table = table[:, kind % 2].rearrange("p r j -> p (r j)")
                part = slice(0, 112) if kind < 2 else slice(0, 56) if kind == 2 else slice(64, 120)
                src = natural(xf0 if kind < 2 else xf2, 0, B)
                for j in range(4):
                    idx = 4 * b + j
                    shift0 = WS - 1 - idx % WS
                    r = src[:, :, idx, :] if kind in (0, 2) else src[:, :, :, idx]
                    o = mm(ps[part, 4 + v % 4, P * j:P * (j + 1)], table[:, shift0 * nh:(shift0 + WS) * nh], r,
                           start=True, stop=True)
                o.then_inc(s["bias_done"], 1)

            for v in range(8):
                relative_bias(v)

            def values(u):
                if u == 0:
                    pe.wait_ge(s["ht0_ready"], NCH)
                    pe.wait_ge(s["ht1_ready"], NCH)
                    pe.wait_ge(s["htw_ready"], 2 * NCH + 4)
                if u in (2, 3):
                    pe.wait_ge(s["blo_ready"], u + 5)
                if u >= 4:
                    pe.wait_ge(s["v_ready"], u - 3)
                for k in range(2):
                    n, c0 = (HALF, HALF * (2 * u + k)) if u < 8 else (PAIR, MAIN + PAIR * (2 * (u - 8) + k))
                    for kc, (wt, r) in enumerate(((wq0, P), (wq1, C - P))):
                        o = mm(ps[0:n, VALUE_BANKS[u % 4], C * k:C * (k + 1)], htw[kc][0:r, c0:c0 + n], wt[:, 2 * C:3 * C],
                               start=(kc == 0), stop=(kc == 1))
                o.then_inc(s["v_done"], 1)

            def values_bias():
                pe.wait_ge(s["wpe_in"], 32)
                pe.wait_ge(s["vb_ready"], 1)
                pe.wait_ge(s["v_ready"], 9)
                mm(ps[:, 2, 0:C], vb[:, 0], wpe0[:], start=True, stop=False)
                mm(ps[:, 2, 0:C], vb[0:C - P, 1], wpe1[:], start=False, stop=True).then_inc(s["vshift_done"], 1)

            for u in range(4):
                values(u)

            def score_piece(h, n):
                k, bank = 12 * h + n, score_bank(n)
                q, kk = qop[h % RING], kop[h % RING]
                if n == 0:
                    pe.wait_ge(op_in[h % RING], operands_loaded(h))
                    if h >= A8:
                        pe.wait_ge(low_in[h % RING], low_biases_loaded(h))
                    pe.wait_ge(const_in[h % RING], 5 * 16)
                if n in (2, 10):
                    pe.wait_ge(s["max_ready"], k)
                elif n == 11:
                    pe.wait_ge(s["shift_ready"], 2 * h + 1)
                elif h and n == 3:
                    pe.wait_ge(s["shift_ready"], 2 * h)
                elif k >= 2:
                    pe.wait_ge(s["max_ready"], k - 1)
                if n < B:
                    for t in range(2):
                        o = mm(ps[0:HALF, bank, WIN * t:WIN * (t + 1)],
                               q[0:R_MASK, WIN * n + HALF * t:WIN * n + HALF * (t + 1)],
                               kk[0:R_MASK, WIN * n:WIN * (n + 1)], start=True, stop=True)
                else:
                    c0 = MAIN + PAIR * (n - B)
                    mm(ps[0:PAIR, bank, 0:PAIR], q[0:R_MAX, c0:c0 + PAIR], kk[0:R_MAX, c0:c0 + PAIR], start=True, stop=True)
                    o = mm(ps[0:PAIR, bank, PAIR:PAIR + WIN], q[0:R_MAX, c0:c0 + PAIR], kk[0:R_MAX, PADS:KCOLS],
                           start=True, stop=True)
                o.then_inc(s["s_done"], 1)

            def main_max_rows(h):
                pe.wait_ge(s["max_ready"], 12 * h + 9)
                pe.wait_ge(s["parts_ready"], 2 * h + 1)
                nc.tensor.transpose(ps[0:4 * B, MAIN_MAX_BANK, 0:HALF], parts[:, h % 2, :],
                                    ident[0:HALF, 0:HALF]).then_inc(s["mt_done"], 1)

            def rest_max_rows(h):
                pe.wait_ge(s["parts_ready"], 2 * h + 2)
                if h + 1 < HEADS:
                    pe.wait_ge(s["max_ready"], 12 * (h + 1) + 1)
                nc.tensor.transpose(ps[0:2 * NP, REST_MAX_BANK, 0:PAIR], parts_rest[:, h % 2, :],
                                    ident[0:PAIR, 0:PAIR]).then_inc(s["mt_done"], 1)

            def weights(h, gi):
                n = 6 * h + gi
                q, kk, b0 = qop[h % RING], kop[h % RING], 2 + 2 * (n % 2)
                if gi == 0:
                    pe.wait_ge(shift_in[h % 2], 16 * (h // 2 + 1))
                if gi == 4:
                    pe.wait_ge(rest_shift_in[h % 2], 16 * (h // 2 + 1))
                if n >= 2:
                    pe.wait_ge(s["exp_done"], n - 1)
                if h == 0 and gi < 2:
                    pe.wait_ge(s["blo_ready"], 16)
                if gi < 4:
                    for i in range(2):
                        img = images_of(gi)[i]
                        for t in range(2):
                            o = mm(ps[0:HALF, b0 + i, WIN * t:WIN * (t + 1)],
                                   kk[:, WIN * img + HALF * t:WIN * img + HALF * (t + 1)],
                                   q[:, WIN * img:WIN * (img + 1)], start=True, stop=True)
                elif gi == 4:
                    for t in range(2):
                        o = mm(ps[0:HALF, b0 + t, 0:B * REST], kk[:, PADS + HALF * t:PADS + HALF * (t + 1)],
                               q[:, MAIN:T], start=True, stop=True)
                else:
                    for p_ in range(NP):
                        c0 = MAIN + PAIR * p_
                        o = mm(ps[0:PAIR, b0, PAIR * p_:PAIR * (p_ + 1)], kk[:, c0:c0 + PAIR], q[:, c0:c0 + PAIR],
                               start=True, stop=True)
                o.then_inc(s["st_done"], 1)

            def sums(h, gi):
                pe.wait_ge(s["exp_done"], 6 * h + gi + 1)
                if gi == 0 and h:
                    pe.wait_ge(s["osb_ready"], 2 * h - 1)
                if gi == 4 and h:
                    pe.wait_ge(s["osb_ready"], 2 * h)
                if gi < 4:
                    for t in range(2):
                        for i in range(2):
                            img = images_of(gi)[i]
                            r0, c0 = 32 * (img // 2), WIN * (img % 2)
                            o = mm(ps[r0:r0 + VD, 6, c0:c0 + WIN], v_main[:, 2 * img + t, h, :],
                                   pm[:, gi % 2, i, WIN * t:WIN * (t + 1)], start=(t == 0), stop=(t == 1))
                elif gi == 4:
                    for t in range(2):
                        for p_ in range(NP):
                            o = mm(ps[32 * p_:32 * p_ + VD, 7, 0:PAIR], v_pad[:, h, :],
                                   ppad[:, t, PAIR * p_:PAIR * (p_ + 1)], start=(t == 0), stop=False)
                else:
                    for p_ in range(NP):
                        o = mm(ps[32 * p_:32 * p_ + VD, 7, 0:PAIR], v_rest[:, p_, h, :],
                               prest[:, PAIR * p_:PAIR * (p_ + 1)], start=False, stop=True)
                o.then_inc(s["pv_done"], 1)

            def spread(k, j):
                n, heads = ((P, A8), (C - P, HEADS - A8))[k]
                if j == 0:
                    pe.wait_ge((s["rd0_in"], s["rd1_in"])[k], (64, 32)[k])
                    pe.wait_ge(s["late_in"], N_LATE)
                    pe.wait_ge(s["sel_ready"], 1)
                    pe.wait_ge(s["shift_ready"], 2 * HEADS)
                if k == 0 and j >= 2:
                    pe.wait_ge(s["on_ready"], j - 1)
                elif k and j < 2:
                    pe.wait_ge(s["res_ready"], NT // 2)
                elif k:
                    pe.wait_ge(s["on_ready"], 4 + j - 1)
                mm(ps[0:n, spread_bank(j), :], sel[0:2 * heads, k, 0:n], rd[0:2 * heads, k, QUAD * j:QUAD * (j + 1)],
                   start=True, stop=True).then_inc(s["bc_done"], 1)

            def shift_of_hidden():
                pe.wait_ge(s["hidden_in"], N_HIDDEN)
                pe.wait_ge(s["exp_done"], 6 * HEADS)
                for m in range(6):
                    mm(ps[:, 2, m:m + 1], w10[:, P * m:P * (m + 1)], vec[:, B2A:B2A + 1], start=True, stop=False)
                    o = mm(ps[:, 2, m:m + 1], w11[0:C - P, P * m:P * (m + 1)], vec[0:C - P, B2B:B2B + 1], start=False, stop=True)
                o.then_inc(s["b1_done"], 1)

            def projection_of_eight(u):
                pe.wait_ge(s["on_ready"], 4)
                if u >= 2:
                    pe.wait_ge(s["res_ready"], u - 1)
                for k in range(2):
                    t = 2 * u + k
                    o = mm(ps[:, u % 2, C * k:C * (k + 1)], on0[:, P * t:P * (t + 1)], wp0[:], start=True, stop=True)
                o.then_inc(s["pr8_done"], 1)

            def scores_for_maxima(g):
                h, n = g // 12 + 1, g % 12
                if n == 10 and h < HEADS:
                    main_max_rows(h)
                if n == 2 and h <= HEADS:
                    rest_max_rows(h - 1)
                if h < HEADS:
                    score_piece(h, n)

            for n in range(12):
                if n == 10:
                    main_max_rows(0)
                score_piece(0, n)
                if n < 6:
                    values(n + 4)
                if n == 5:
                    values_bias()
                if n >= 6:
                    relative_bias(n + 2)
            for v in (14, 15):
                relative_bias(v)
            for g in range(LEAD):
                scores_for_maxima(g)
            for h in range(HEADS):
                for gi in range(6):
                    g = 12 * h + 2 * gi + LEAD
                    weights(h, gi)
                    scores_for_maxima(g)
                    if gi:
                        sums(h, gi - 1)
                    elif h:
                        sums(h - 1, 5)
                    scores_for_maxima(g + 1)
                    if h == HEADS - 1:
                        if gi < 4:
                            spread(0, gi)
                        elif gi == 4:
                            projection_of_eight(0)
                        else:
                            projection_of_eight(1)
            sums(HEADS - 1, 5)
            for u in range(2, NT // 2):
                projection_of_eight(u)
            shift_of_hidden()

            def projection(c):
                for u in (2 * c, 2 * c + 1):
                    if u == 0:
                        pe.wait_ge(s["b1_ready"], 1)
                    if u >= 4:
                        pe.wait_ge(s["x2_ready"], u - 3)
                    pe.wait_ge(s["on_ready"], 4 + c + 1)
                    for k in range(2):
                        t = 2 * u + k
                        o = mm(ps[:, 2 + u % 4, C * k:C * (k + 1)], on1[:, P * t:P * (t + 1)], wp1[:], start=True, stop=True)
                    o.then_inc(s["pr_done"], 1)

            spread(1, 0)
            spread(1, 1)
            projection(0)
            spread(1, 2)
            projection(1)
            spread(1, 3)
            projection(2)

            def late_src(c, k):
                return xn2[:, 4 * c + k]

            def second_transposes(c):
                if c == 0:
                    pe.wait_ge(s["osb_ready"], 2 * HEADS)
                    pe.wait_ge(s["on_ready"], 8)
                pe.wait_ge(s["xn2_ready"], 4 * (c + 1))
                transposes(c, late_src, s["tp2_done"], (6, 0), (s["h2h_ready"], s["h2l_ready"]), 2)

            def hidden(c):
                pe.wait_ge(s["h2h_ready"], 2 * (c + 1))
                pe.wait_ge(s["h2l_ready"], 2 * (c + 1))
                for m in range(6):
                    n = 6 * c + m
                    if n == 0:
                        pe.wait_ge(s["w1_split"], 2)
                        pe.wait_ge(s["x2_ready"], 6)
                    if n >= 2:
                        pe.wait_ge(s["gl_ready"], n - 1)
                    terms = ((w10h, h2h[:, c % 2]), (w10l, h2h[:, c % 2]), (w10h, h2l[:, c % 2]),
                             (w11s, h2s[:, c % 2]), (w11l, h2s[0:C - P, c % 2]))
                    for i, (wt, ht) in enumerate(terms):
                        o = mm(ps[:, 2 + n % 2, :], wt[:, P * m:P * (m + 1)], ht, start=(i == 0), stop=(i == 4))
                    o.then_inc(s["m1_done"], 1)
                    if m == 1 and c + 1 < NCH:
                        second_transposes(c + 1)

            def second_layer(c):
                pe.wait_ge(s["gl_ready"], 6 * (c + 1))
                for u in (2 * c, 2 * c + 1):
                    if u == 0:
                        pe.wait_ge(s["x2_ready"], NT // 2)
                    if u >= 2:
                        pe.wait_ge(s["y_ready"], u - 1)
                    for k in range(2):
                        t = 2 * (u % 2) + k
                        for m in range(6):
                            o = mm(ps[:, 4 + u % 2, C * k:C * (k + 1)], gl[:, c % 2, m, P * t:P * (t + 1)], w2t[:, m],
                                   start=(m == 0), stop=(m == 5))
                    o.then_inc(s["m2_done"], 1)

            second_transposes(0)
            projection(3)
            for c in range(NCH):
                hidden(c)
                if c:
                    second_layer(c - 1)
            second_layer(NCH - 1)


def _constants():
    import numpy as np
    k = np.zeros((ROWS, 512), np.float32)
    pos = [(r, c, -1) for r in range(WS) for c in range(WS)]
    of_image = [(r, c, 0) for r in range(WS) for c in range(W - WS)]
    of_image += [(r, c % WS, 1 if c < WS else 2) for r in range(H - WS) for c in range(W)]
    cols = list(pos)
    for par in range(2):
        cols += [(r, c, w + 3 * par) for r, c, w in of_image]
    cols += [(r, c, -2) for r, c, _ in pos]
    for n, (r, c, cls) in enumerate(cols):
        for row in (R_BIAS + 4 * r, R_BIAS + 4 * c + 2):
            k[row:row + 2, n] = 1.0
        for j in range(6):
            if cls >= 0:
                allowed = j == cls
            elif cls == -2:
                real = ((c < 2), (r < 2), (r < 2 and c < 2))[j % 3]
                allowed = not real
            else:
                allowed = True
            k[R_MASK + j, n] = 0.0 if allowed else MASKED
        k[R_MAX:R_MAX + 2, n] = 1.0
    q = np.zeros((ROWS, 512), np.float32)
    for n, (_, _, cls) in enumerate(cols[WIN:WIN + PAIR]):
        q[R_MASK + cls, 2 * WIN + n] = 1.0
    return k[R_BIAS:], q[R_MASK:]


def kernel(**inputs):
    import numpy as np
    import concourse.bacc as _bacc
    from concourse import mybir as _mybir
    from concourse.bass_utils import run_bass_kernel_spmd as _run

    i = {n.replace("L0_conv_", ""): np.ascontiguousarray(a) for n, a in inputs.items()}
    kconst, qconst = _constants()
    vectors = np.zeros((P, 32), np.float32)
    for n, name in ((0, "ln1_g"), (1, "ln1_b"), (4, "ln2_g"), (5, "ln2_b")):
        vectors[:, n] = i[name][:P]
        vectors[:C - P, n + 2] = i[name][P:]
    vectors[P - (C - P):, 6] = i["ln2_g"][P:]
    vectors[:, 8] = i["qkv_b"][0:P]
    vectors[:, 9] = i["qkv_b"][C:C + P]
    vectors[:64, 10] = i["qkv_b"][P:C]
    vectors[64:, 10] = i["qkv_b"][C + P:2 * C]
    vectors[:, 11:17] = i["mlp_b1"].reshape(6, P).T
    vectors[:, 17] = 1.0
    vectors[:, 18] = KD ** -0.5
    vectors[:64, 19] = 1.0
    vectors[64:, 19] = KD ** -0.5
    for h in range(A8):
        vectors[KD * h:KD * (h + 1), 24 + h] = 1.0
    vectors[:, 20] = i["qkv_b"][2 * C:2 * C + P]
    vectors[:C - P, 21] = i["qkv_b"][2 * C + P:]
    rows = np.stack([i["proj_b"], i["mlp_b2"]])
    selector = np.zeros((2 * A8, 2, P), np.float32)
    for h in range(A8):
        selector[h::A8, 0, KD * h:KD * (h + 1)] = 1.0
    for h in range(4):
        selector[h:8:4, 1, KD * h:KD * (h + 1)] = 1.0
    rel = np.ascontiguousarray(np.stack([i["rel_h"][::-1].T, i["rel_w"][::-1].T], axis=1))
    arrays = {"x": i["x"], "qkv_w": i["qkv_w"], "proj_w": i["proj_w"], "selector": selector,
              "mlp_w1": i["mlp_w1"], "mlp_w2": i["mlp_w2"],
              "vectors": vectors, "rows": rows, "rel": rel, "kconst": kconst, "qconst": qconst,
              "ident_in": np.eye(P, dtype=np.float32)}
    nc = _bacc.Bacc("TRN2", target_bir_lowering=False, num_devices=1)
    args = {n: nc.dram_tensor(f"in_{n}", a.shape, _mybir.dt.from_np(a.dtype), kind="ExternalInput").ap()
            for n, a in arrays.items()}
    args["out"] = nc.dram_tensor("out_0", (B, H, W, C), _mybir.dt.float32, kind="ExternalOutput").ap()
    window_attention_block(nc, **args)
    r = _run(nc, [{f"in_{n}": a for n, a in arrays.items()}], core_ids=[0])
    return r.results[0]["out_0"]
```
